# Optimizing a Trainium2 kernel written in Bass

```python
import numpy as np
import jax
import jax.numpy as jnp

def _softmax(x, axis=-1):
    return jax.nn.softmax(x, axis=axis)

def _gelu(x):
    return jax.nn.gelu(x, approximate=True)

def _silu(x):
    return jax.nn.silu(x)

def _sigmoid(x):
    return jax.nn.sigmoid(x)

def _layernorm(x, axis=-1, eps=1e-05):
    m = jnp.mean(x, axis=axis, keepdims=True)
    v = jnp.var(x, axis=axis, keepdims=True)
    return (x - m) / jnp.sqrt(v + eps)

def _scatter_add(tgt, idx, src, axis=0):
    return tgt.at[idx].add(src)

def _segment_sum(src, seg, n):
    return jax.ops.segment_sum(src, seg, n)
kernel_name = 'mk_xattn_ffn_d1_seqx_r2_837a37'

def setup_inputs(seed: int=0):
    np.random.seed(seed)
    _w = jnp.asarray

    def _rec_inputs():
        import jax
        import jax.numpy as jnp
        _rk = jax.random.key(seed)
        x = 4.136e-05 + 0.9999 * jax.random.normal(jax.random.fold_in(_rk, 1), (4, 1024, 1024), jnp.float32)
        _lenS = 1024 - jax.random.randint(jax.random.fold_in(_rk, 7), (4,), 0, max(1, 1024 // 4) + 1, jnp.int32)
        _lenS2 = 1024 - jax.random.randint(jax.random.fold_in(_rk, 8), (4,), 0, max(1, 1024 // 4) + 1, jnp.int32)
        _ctx_1024P = jax.random.normal(jax.random.fold_in(_rk, 11), (4, 16, 512), jnp.float32)
        _ctx_1024c = jax.random.dirichlet(jax.random.fold_in(_rk, 511), 0.3 * jnp.ones((16,), jnp.float32), (4, 1024))
        _ctx_1024t = jnp.einsum('bsk,bkd->bsd', _ctx_1024c, _ctx_1024P)
        _ctx_1024t = _ctx_1024t * jax.lax.rsqrt(jnp.mean(jnp.square(_ctx_1024t)) + 1e-12) * 0.953939
        ctx_1024 = -0.000292821 + 1.00034 * (_ctx_1024t + 0.3 * jax.random.normal(jax.random.fold_in(_rk, 611), (4, 1024, 512), jnp.float32))
        return (x, ctx_1024)
    x, ctx_1024 = _rec_inputs()

    def _L0_xattn_setup():
        import jax, jax.numpy as jnp
        import numpy as np
        import math
        B, L, DM = (2, 1024, 512)
        DS, DC, EXP = (16, 4, 2)
        DI = EXP * DM
        DR = math.ceil(DM / 16)
        DT_MIN, DT_MAX, DT_FLOOR = (0.001, 0.1, 0.0001)

        def _ssm_forward(hidden_states, z, in_proj_w, conv_w, conv_b, x_proj_w, dt_proj_w, dt_proj_b, A_log, D):
            b = hidden_states.shape[0]
            x = jnp.einsum('ed,bld->bel', in_proj_w, hidden_states)
            xp = jnp.pad(x, ((0, 0), (0, 0), (DC - 1, 0)))
            xc = jax.lax.conv_general_dilated(xp, conv_w[:, None, :], window_strides=(1,), padding='VALID', dimension_numbers=('NCH', 'OIH', 'NCH'), feature_group_count=DI)
            u = jax.nn.silu(xc + conv_b[None, :, None])
            x_dbl = jnp.einsum('ke,bel->bkl', x_proj_w, u)
            dt_lo = x_dbl[:, :DR]
            Bm = x_dbl[:, DR:DR + DS]
            Cm = x_dbl[:, DR + DS:]
            delta = jax.nn.softplus(jnp.einsum('er,brl->bel', dt_proj_w, dt_lo) + dt_proj_b[None, :, None])
            A = -jnp.exp(A_log)

            def step(state, xs):
                d_t, B_t, C_t, u_t = xs
                dA = jnp.exp(d_t[..., None] * A)
                state = state * dA + (d_t * u_t)[..., None] * B_t[:, None, :]
                y_t = jnp.einsum('ben,bn->be', state, C_t)
                return (state, y_t)
            xs = (jnp.moveaxis(delta, -1, 0), jnp.moveaxis(Bm, -1, 0), jnp.moveaxis(Cm, -1, 0), jnp.moveaxis(u, -1, 0))
            state0 = jnp.zeros((b, DI, DS), delta.dtype)
            _, ys = jax.lax.scan(step, state0, xs)
            y = jnp.moveaxis(ys, 0, -1)
            y = y + D[None, :, None] * u
            y = y * jax.nn.silu(z)
            return jnp.swapaxes(y, 1, 2)
        key = jax.random.key(seed)
        ks = jax.random.split(key, 8)
        hidden_states = jax.random.normal(ks[0], (B, L, DM), jnp.float32)
        z = jax.random.normal(ks[1], (B, DI, L), jnp.float32)
        in_proj_w = jax.random.normal(ks[2], (DI, DM), jnp.float32) * DM ** (-0.5)
        conv_w = jax.random.normal(ks[3], (DI, DC), jnp.float32) * DC ** (-0.5)
        conv_b = jnp.zeros((DI,), jnp.float32)
        x_proj_w = jax.random.normal(ks[4], (DR + 2 * DS, DI), jnp.float32) * DI ** (-0.5)
        dt_std = DR ** (-0.5)
        dt_proj_w = jax.random.uniform(ks[5], (DI, DR), jnp.float32, -dt_std, dt_std)
        dt = jnp.exp(jax.random.uniform(ks[6], (DI,), jnp.float32) * (math.log(DT_MAX) - math.log(DT_MIN)) + math.log(DT_MIN))
        dt = jnp.clip(dt, DT_FLOOR)
        dt_proj_b = dt + jnp.log(-jnp.expm1(-dt))
        A_log = jnp.log(jnp.broadcast_to(jnp.arange(1, DS + 1, dtype=jnp.float32), (DI, DS)))
        D = jnp.ones((DI,), jnp.float32)
        return dict(hidden_states=hidden_states, z=z, in_proj_w=in_proj_w, conv_w=conv_w, conv_b=conv_b, x_proj_w=x_proj_w, dt_proj_w=dt_proj_w, dt_proj_b=dt_proj_b, A_log=A_log, D=D)
    _L0_xattn_all = _L0_xattn_setup()
    _L0_xattn_in = {k: v for k, v in _L0_xattn_all.items() if k in ('in_proj_w', 'conv_w', 'conv_b', 'x_proj_w', 'dt_proj_w', 'dt_proj_b', 'A_log', 'D')}
    del _L0_xattn_all

    def _L0_ffn_setup():
        import jax, jax.numpy as jnp
        import numpy as np
        B, S, D, E, TOPK, H = (8, 1024, 1024, 8, 2, 16)
        DH = D // H
        FH = D // H
        ROUTE_LEN = 1024
        key = jax.random.key(seed)
        ks = jax.random.split(key, 8)
        s = 0.02
        return {'x': jax.random.normal(ks[0], (B, S, D), jnp.float32), 'switch_w': jax.random.normal(ks[1], (E, D * ROUTE_LEN), jnp.float32) * s, 'switch_b': jnp.zeros((E,), jnp.float32), 'w1': jax.random.normal(ks[2], (E, FH, DH), jnp.float32) * s, 'b1': jnp.zeros((E, FH), jnp.float32), 'w2': jax.random.normal(ks[3], (E, DH, FH), jnp.float32) * s, 'b2': jnp.zeros((E, DH), jnp.float32), 'w3': jax.random.normal(ks[4], (D, D), jnp.float32) * s, 'b3': jnp.zeros((D,), jnp.float32)}
    _L0_ffn_all = _L0_ffn_setup()
    _L0_ffn_in = {k: v for k, v in _L0_ffn_all.items() if k in ('switch_w', 'switch_b', 'w1', 'b1', 'w2', 'b2', 'w3', 'b3')}
    del _L0_ffn_all
    return {'x': x, 'ctx_1024': ctx_1024, 'L0_xattn_in_proj_w': _L0_xattn_in['in_proj_w'], 'L0_xattn_conv_w': _L0_xattn_in['conv_w'], 'L0_xattn_conv_b': _L0_xattn_in['conv_b'], 'L0_xattn_x_proj_w': _L0_xattn_in['x_proj_w'], 'L0_xattn_dt_proj_w': _L0_xattn_in['dt_proj_w'], 'L0_xattn_dt_proj_b': _L0_xattn_in['dt_proj_b'], 'L0_xattn_A_log': _L0_xattn_in['A_log'], 'L0_xattn_D': _L0_xattn_in['D'], 'L0_ffn_switch_w': _L0_ffn_in['switch_w'], 'L0_ffn_switch_b': _L0_ffn_in['switch_b'], 'L0_ffn_w1': _L0_ffn_in['w1'], 'L0_ffn_b1': _L0_ffn_in['b1'], 'L0_ffn_w2': _L0_ffn_in['w2'], 'L0_ffn_b2': _L0_ffn_in['b2'], 'L0_ffn_w3': _L0_ffn_in['w3'], 'L0_ffn_b3': _L0_ffn_in['b3']}

def reference(x, ctx_1024, L0_xattn_in_proj_w, L0_xattn_conv_w, L0_xattn_conv_b, L0_xattn_x_proj_w, L0_xattn_dt_proj_w, L0_xattn_dt_proj_b, L0_xattn_A_log, L0_xattn_D, L0_ffn_switch_w, L0_ffn_switch_b, L0_ffn_w1, L0_ffn_b1, L0_ffn_w2, L0_ffn_b2, L0_ffn_w3, L0_ffn_b3):
    import jax
    import jax.numpy as jnp

    def _L0_xattn_ref(hidden_states, z, in_proj_w, conv_w, conv_b, x_proj_w, dt_proj_w, dt_proj_b, A_log, D):
        import jax, jax.numpy as jnp
        import numpy as np
        import math
        B, L, DM = (2, 1024, 512)
        DS, DC, EXP = (16, 4, 2)
        DI = EXP * DM
        DR = math.ceil(DM / 16)
        DT_MIN, DT_MAX, DT_FLOOR = (0.001, 0.1, 0.0001)

        def _ssm_forward(hidden_states, z, in_proj_w, conv_w, conv_b, x_proj_w, dt_proj_w, dt_proj_b, A_log, D):
            b = hidden_states.shape[0]
            x = jnp.einsum('ed,bld->bel', in_proj_w, hidden_states)
            xp = jnp.pad(x, ((0, 0), (0, 0), (DC - 1, 0)))
            xc = jax.lax.conv_general_dilated(xp, conv_w[:, None, :], window_strides=(1,), padding='VALID', dimension_numbers=('NCH', 'OIH', 'NCH'), feature_group_count=DI)
            u = jax.nn.silu(xc + conv_b[None, :, None])
            x_dbl = jnp.einsum('ke,bel->bkl', x_proj_w, u)
            dt_lo = x_dbl[:, :DR]
            Bm = x_dbl[:, DR:DR + DS]
            Cm = x_dbl[:, DR + DS:]
            delta = jax.nn.softplus(jnp.einsum('er,brl->bel', dt_proj_w, dt_lo) + dt_proj_b[None, :, None])
            A = -jnp.exp(A_log)

            def step(state, xs):
                d_t, B_t, C_t, u_t = xs
                dA = jnp.exp(d_t[..., None] * A)
                state = state * dA + (d_t * u_t)[..., None] * B_t[:, None, :]
                y_t = jnp.einsum('ben,bn->be', state, C_t)
                return (state, y_t)
            xs = (jnp.moveaxis(delta, -1, 0), jnp.moveaxis(Bm, -1, 0), jnp.moveaxis(Cm, -1, 0), jnp.moveaxis(u, -1, 0))
            state0 = jnp.zeros((b, DI, DS), delta.dtype)
            _, ys = jax.lax.scan(step, state0, xs)
            y = jnp.moveaxis(ys, 0, -1)
            y = y + D[None, :, None] * u
            y = y * jax.nn.silu(z)
            return jnp.swapaxes(y, 1, 2)
        return _ssm_forward(hidden_states, z, in_proj_w, conv_w, conv_b, x_proj_w, dt_proj_w, dt_proj_b, A_log, D)

    def _L0_ffn_ref(x, switch_w, switch_b, w1, b1, w2, b2, w3, b3):
        import jax, jax.numpy as jnp
        import numpy as np
        B, S, D, E, TOPK, H = (8, 1024, 1024, 8, 2, 16)
        DH = D // H
        FH = D // H
        ROUTE_LEN = 1024
        b, s, d = x.shape
        x0 = x[:, :ROUTE_LEN].reshape(b, -1)
        logits = x0 @ switch_w.T + switch_b
        probs = jax.nn.softmax(logits, axis=-1)
        gate, top_idx = jax.lax.top_k(probs, TOPK)
        xh = x.reshape(b, s, H, DH).transpose(0, 2, 1, 3)
        w1s, b1s = (w1[top_idx], b1[top_idx])
        w2s, b2s = (w2[top_idx], b2[top_idx])
        h = jnp.einsum('bhsd,bkfd->bkhsf', xh, w1s) + b1s[:, :, None, None, :]
        h = jax.nn.gelu(h, approximate=False)
        o = jnp.einsum('bkhsf,bkdf->bkhsd', h, w2s) + b2s[:, :, None, None, :]
        o = (o * gate[:, :, None, None, None]).sum(axis=1)
        o = o.transpose(0, 2, 1, 3).reshape(b, s, d)
        out = x + o
        return out @ w3.T + b3
    x = x + _L0_xattn_ref(ctx_1024, _layernorm(x, axis=-1), L0_xattn_in_proj_w, L0_xattn_conv_w, L0_xattn_conv_b, L0_xattn_x_proj_w, L0_xattn_dt_proj_w, L0_xattn_dt_proj_b, L0_xattn_A_log, L0_xattn_D)
    x = x + _L0_ffn_ref(_layernorm(x, axis=-1), L0_ffn_switch_w, L0_ffn_switch_b, L0_ffn_w1, L0_ffn_b1, L0_ffn_w2, L0_ffn_b2, L0_ffn_w3, L0_ffn_b3)
    return x

_drawn_inputs = setup_inputs


def setup_inputs(seed=0):
    import zlib

    import numpy as np

    out = dict(_drawn_inputs(seed))
    spreads = {'L0_xattn_conv_b': (0.0, 0.1),
     'L0_xattn_D': (1.0, 0.2),
     'L0_ffn_switch_b': (0.0, 0.1),
     'L0_ffn_b1': (0.0, 0.8),
     'L0_ffn_b2': (0.0, 0.1),
     'L0_ffn_b3': (0.0, 0.1)}
    factors = {'L0_xattn_dt_proj_w': 4.951, 'L0_ffn_w1': 8.0, 'L0_ffn_w2': 6.91}
    for name, (base, spread) in spreads.items():
        noise = np.random.default_rng([zlib.crc32(name.encode()), seed]).standard_normal(out[name].shape)
        drawn = base * np.exp(spread * noise) if base else spread * noise
        out[name] = jnp.asarray(drawn.astype(out[name].dtype))
    for name, factor in factors.items():
        out[name] = (out[name] * factor).astype(out[name].dtype)
    return out
```

```python
from contextlib import ExitStack

import concourse.bass as bass
from concourse import mybir

F32 = mybir.dt.float32
U32 = mybir.dt.uint32
ALU = mybir.AluOpType
ACT = mybir.ActivationFunctionType
AX = mybir.AxisListType

P = 128
NB, L, DI, DM = 4, 1024, 1024, 512
T = 512
TH = L // T
TB = T // P
J = DI // P
N = 16
DR = 32
DC = 4
E = 8
HD = 64
DK = DM // P
EPS = 1e-5
PAIRS = N // 2
CH = T + DC - 1
SD = 128
QD = 256
NQ = DI // QD

P1_E, P2_E, S_E, F1_E = (J // 2, J // 2), (1, 0), (J, J), (TB // 2, TB // 2)
F2_E = (0, 1)
F3T_E, F3E_E, F3W_E = (TB, TB), (2 * J, J), (NQ * TB // 2, NQ * TB // 2)
TH_E = tuple(P1_E[s] + P2_E[s] + S_E[s] + F1_E[s] for s in (0, 1))
F3_E = tuple(F3T_E[s] + F3E_E[s] + F3W_E[s] for s in (0, 1))
B_E = tuple(TH * TH_E[s] + F2_E[s] + TH * F3_E[s] for s in (0, 1))


def front(s, b, th):
    return b * B_E[s] + th * TH_E[s]


def back(s, b, th):
    return b * B_E[s] + TH * TH_E[s] + F2_E[s] + th * F3_E[s]


def build(nc, x, ctxT, w_inT, conv_w, conv_b, x_projT, dt_projT, dt_b, A_log, D, sw, sw_b,
          w1T, b1, w2T, b2, w3T, b3, out):
    x1_d = nc.dram_tensor("x1_scratch", (NB, L, DI), F32, kind="Internal").ap()
    bc_d = nc.dram_tensor("bc_scratch", (NB * TH, 2 * N, T), F32, kind="Internal").ap()

    with ExitStack() as ctx:
        def sb(name, shape, dt=F32):
            return ctx.enter_context(nc.sbuf_tensor(name, shape, dt))

        counts = []

        def sem(name, start=0):
            s = ctx.enter_context(nc.semaphore(name))
            counts.append((s, 1 + start))
            return s

        ident = sb("ident", [P, P])
        ones = sb("ones", [P, P])
        diag = sb("diag", [P, 32])
        iota = sb("iota", [P, E])
        half = sb("half", [P, 2])
        xpw = sb("xpw", [P, J, DR + 2 * N])
        cw = sb("cw", [P, J, DC])
        cb = sb("cb", [P, J])
        Dv = sb("Dv", [P, J])
        Av = sb("Av", [P, J * N])
        b1c = sb("b1c", [P, E])
        b2c = sb("b2c", [P, E])
        swb = sb("swb", [P, E])
        b3r = sb("b3r", [P, DI])
        r1 = sb("r1", [P, NB * J])
        nm1 = sb("nm1", [P, NB * J])
        mv1 = sb("mv1", [P, NB * J, 2])
        ctxs = sb("ctxs", [P, DK, T])
        win = sb("win", [P, 2, DK, P])
        xpad = sb("xpad", [P, CH])
        halo = sb("halo", [P, J, DC - 1])
        cacc = sb("cacc", [P, T])
        u = sb("u", [P, J, T])
        dtaug = sb("dtaug", [DR + 1, T])
        Bb = sb("Bb", [P, N, T])
        Cb = sb("Cb", [P, N, T])
        dtall = sb("dtall", [DR + 1, DI])
        dtw = sb("dtw", [DR + 1, 2, P])
        sp = sb("sp", [P, T])
        delta = sb("delta", [P, 2, T])
        dA = sb("dA", [P, 2, T])
        h = sb("h", [P, 4, T])
        prod = sb("prod", [P, 4, T])
        state = sb("state", [P, J * N])
        Du = sb("Du", [P, T])
        xz = sb("xz", [P, T])
        szT = sb("szT", [P, TB, P])
        xt = sb("xt", [P, TB, P])
        yg = sb("yg", [P, 2, TB, P])
        row = sb("row", [P, 2, DI])
        xn = sb("xn", [P, DI])
        bst = sb("bst", [P, 2, 2, 6])
        mv = sb("mv", [P, 2, 2])
        r2 = sb("r2", [P, TH * TB])
        nm2 = sb("nm2", [P, TH * TB])
        sww = sb("sww", [P, 2, E, SD])
        lgm = sb("lgm", [P, E, 32])
        lgr = sb("lgr", [P, TH * TB, E])
        rt = sb("rt", [P, 8, E])
        idx = sb("idx", [P, E], U32)
        hot = sb("hot", [P, 2, E])
        w1s = sb("w1s", [P, 2, P])
        w2s = sb("w2s", [P, 2, P])
        b1s = sb("b1s", [P, 2])
        b2s = sb("b2s", [P, 4])
        xT = sb("xT", [P, J, T])
        hs = sb("hs", [P, 2, T])
        w3q = sb("w3q", [P, J, QD])
        res = sb("res", [P, TB, QD])
        bcs = xpad[DR:DR + 2 * N, 0:T]
        w12 = hs[:].rearrange("p i (e f) -> p i e f", e=E)
        wt = xn[:, 0:E * HD].rearrange("p (e f) -> p e f", e=E)

        duB = ctx.enter_context(nc.psum_tensor("duB", [P, 4, T], F32))
        du = ctx.enter_context(nc.psum_tensor("du", [P, T], F32))
        yT = ctx.enter_context(nc.psum_tensor("yT", [P, TB, P], F32))
        dense = ctx.enter_context(nc.psum_tensor("dense", [P, 2, T], F32))

        const_loaded = sem("const_loaded")
        ctx_loaded = sem("ctx_loaded")
        win_loaded = [sem(f"win_loaded{p}") for p in (0, 1)]
        xt_loaded = sem("xt_loaded")
        experts_loaded = sem("experts_loaded")
        xz_loaded = sem("xz_loaded")
        bc_stored = sem("bc_stored")
        bc_loaded = sem("bc_loaded")
        x1_stored = [sem(f"x1_stored{p}") for p in (0, 1)]
        row_loaded = [sem(f"row_loaded{p}") for p in (0, 1)]
        sww_loaded = [sem(f"sww_loaded{p}") for p in (0, 1)]
        w3_loaded = sem("w3_loaded")
        out_stored = sem("out_stored")
        set_up = sem("set_up")
        ident_step = sem("ident_step")
        bn_step = sem("bn_step")
        mv1_step = sem("mv1_step")
        zeroed = sem("zeroed")
        masks = sem("masks")
        a_ready = sem("a_ready")
        ln1_step = sem("ln1_step")
        row_read = sem("row_read", start=1)
        evac = [sem(f"evac{s}") for s in (0, 1)]
        xin_done = sem("xin_done", start=1)
        conv_step = sem("conv_step")
        u_done = sem("u_done")
        xdbl_done = sem("xdbl_done")
        dtrows_done = sem("dtrows_done")
        dtw_done = sem("dtw_done")
        v_done = sem("v_done", start=1)
        sp_step = sem("sp_step")
        du_done = sem("du_done")
        dA_done = sem("dA_done")
        duB_done = sem("duB_done")
        h_done = sem("h_done", start=1)
        saved = sem("saved")
        prod_done = sem("prod_done", start=1)
        prod_summed = sem("prod_summed", start=1)
        Du_done = sem("Du_done")
        zn_done = sem("zn_done")
        zT_done = sem("zT_done")
        yg_done = sem("yg_done")
        x1_done = sem("x1_done", start=1)
        mv_step = sem("mv_step")
        rs_done = sem("rs_done")
        nm_done = sem("nm_done")
        xn_done = sem("xn_done", start=1)
        sw_used = sem("sw_used", start=1)
        lgr_done = sem("lgr_done")
        lg_done = sem("lg_done")
        route_step = sem("route_step")
        pexp_done = sem("pexp_done")
        top_step = sem("top_step")
        wt_step = sem("wt_step")
        sel_half = sem("sel_half")
        sel_step = sem("sel_step")
        tr_done = sem("tr_done")
        hid_done = sem("hid_done")
        o_done = sem("o_done")
        w3_done = sem("w3_done")
        res_loaded = sem("res_loaded")
        rowb_done = sem("rowb_done")

        CONSTS = 13
        settled = sem("settled")
        for s_, start in counts:
            nc.sync.sem_inc(s_, start)
        nc.all_engine_barrier()
        block = ctx.enter_context(nc.Block())

        def settle(eng):
            eng.sem_inc(settled, 1)

        def steps(eng, body):
            settle(eng)
            with eng.Fori(0, J // 2) as j2:
                for p in (0, 1):
                    body(2 * j2 + p, j2, p)

        def rows(eng, body):
            settle(eng)
            with eng.Fori(0, TB // 2) as k2:
                for p in (0, 1):
                    body(2 * k2 + p, k2, p)

        @block.sync
        def _(sp_):
            e = sp_
            with nc.allow_non_contiguous_dma(reason="small weights, once"):
                for dst, src in (
                    (xpw[:], x_projT.rearrange("(j p) k -> p j k", p=P)),
                    (cw[:], conv_w.rearrange("(j p) k -> p j k", p=P)),
                    (cb[:], conv_b.rearrange("(j p) -> p j", p=P)),
                    (Dv[:], D.rearrange("(j p) -> p j", p=P)),
                    (Av[:].rearrange("p (j n) -> p j n", n=N), A_log.rearrange("(j p) n -> p j n", p=P)),
                    (b1c[0:HD], b1.rearrange("e f -> f e")),
                    (b1c[HD:P], b1.rearrange("e f -> f e")),
                    (b2c[0:HD], b2.rearrange("e d -> d e")),
                    (b2c[HD:P], b2.rearrange("e d -> d e")),
                    (swb[:], sw_b.partition_broadcast(P)),
                    (b3r[:], b3.partition_broadcast(P)),
                    (dtall[0:DR], dt_projT),
                    (dtall[DR:DR + 1], dt_b),
                ):
                    e.dma_start(dst, src).then_inc(const_loaded, 16)
            xr = x.rearrange("b (j p) d -> (b j) p d", p=P)
            with e.Fori(0, NB * J // 2) as i2:
                for p in (0, 1):
                    e.wait_ge(row_read, 1 + 2 * i2 + p)
                    settle(e)
                    e.dma_start(row[:, p, :], xr[bass.ds(2 * i2 + p, 1)].rearrange("o p d -> p (o d)")) \
                        .then_inc(row_loaded[p], 16)
            e.wait_ge(row_read, 1 + NB * J + 1)
            settle(e)

            with e.Fori(0, NB) as b:
                with e.Fori(0, TH) as th:
                    c = TH * b + th
                    e.wait_ge(xin_done, 1 + J * c + 1)
                    settle(e)
                    e.dma_start(ctxs[:], ctxT[bass.ds(b, 1), :, bass.ds(th * T, T)]
                                .rearrange("o (k p) t -> p (o k) t", p=P)).then_inc(ctx_loaded, 16)

                    def in_proj_weights(j, j2, p):
                        e.wait_ge(xin_done, 1 + J * c + 2 * j2 + p)
                        settle(e)
                        e.dma_start(win[:, p], w_inT[:, bass.ds(j * P, P)].rearrange("(k p) e -> p k e", p=P)) \
                            .then_inc(win_loaded[p], 16)
                    steps(e, in_proj_weights)

                    e.wait_ge(evac[0], 1 + front(0, b, th) + P1_E[0] + P2_E[0])
                    settle(e)
                    e.dma_start(bc_d[bass.ds(c, 1)].rearrange("o n t -> (o n) t"), bcs) \
                        .then_inc(bc_stored, 16)
                    e.wait_ge(bc_stored, 1 + 16 * (c + 1))
                    e.wait_ge(duB_done, 1 + PAIRS * J * c)
                    settle(e)
                    e.wait_ge(prod_done, 1 + PAIRS * J * c + 1)
                    settle(e)
                    for half_, dst in ((0, Bb), (1, Cb)):
                        e.dma_start(dst[:], bc_d[bass.ds(c, 1), N * half_:N * half_ + N, :]
                                    .rearrange("o n t -> (o n) t").partition_broadcast(P)) \
                            .then_inc(bc_loaded, 16)

                    def scan_loads(j, j2, p):
                        g = J * c + 2 * j2 + p
                        e.wait_ge(zT_done, 1 + g)
                        settle(e)
                        e.dma_start(xz[:], x[bass.ds(b, 1), bass.ds(j * P, P), bass.ds(th * T, T)]
                                    .rearrange("o e t -> (o e) t")).then_inc(xz_loaded, 16)
                        e.wait_ge(x1_done, 1 + g + 1)
                        settle(e)
                        e.dma_start(xt[:], x[bass.ds(b, 1), bass.ds(th * T, T), bass.ds(j * P, P)]
                                    .rearrange("o (k p) e -> p (o k) e", p=P)).then_inc(xt_loaded, 16)
                        e.wait_ge(x1_done, 1 + g + 2)
                        settle(e)
                        e.dma_start(x1_d[bass.ds(b, 1), bass.ds(th * T, T), bass.ds(j * P, P)]
                                    .rearrange("o (k p) e -> p (o k) e", p=P), yg[:, p]).then_inc(x1_stored[p], 16)
                    steps(e, scan_loads)

                    for p in (0, 1):
                        e.wait_ge(x1_stored[p], 1 + 16 * (J // 2) * (c + 1))
                        settle(e)

                    def logit_loads(k, k2, p):
                        f = TB * c + 2 * k2 + p
                        e.wait_ge(xn_done, 1 + 2 * TH * TB * b + TB * th + 2 * k2 + p)
                        settle(e)
                        e.dma_start(row[:, p, :], x1_d[bass.ds(b, 1), bass.ds(th * T + k * P, P), :]
                                    .rearrange("o p d -> p (o d)")).then_inc(row_loaded[p], 16)
                        for q in range(DI // SD):
                            e.wait_ge(sw_used, 1 + f * (DI // SD) + q)
                            settle(e)
                            e.dma_start(sww[:, q % 2], sw[:, bass.ds(th * T + k * P, P), q * SD:(q + 1) * SD]
                                        .rearrange("e p d -> p e d")).then_inc(sww_loaded[q % 2], 16)
                    rows(e, logit_loads)

                e.wait_ge(o_done, 1 + TH * J * b)
                settle(e)
                for i, w in ((0, w1T), (1, w2T)):
                    for lo in (0, HD):
                        e.dma_start(w12[lo:lo + HD, i], w.rearrange("e r c -> r e c")).then_inc(experts_loaded, 16)

                with e.Fori(0, TH) as th:
                    c = TH * b + th

                    def back_rows(k, k2, p):
                        e.wait_ge(xn_done, 1 + 2 * TH * TB * b + TB * (TH + th) + 2 * k2 + p)
                        settle(e)
                        e.dma_start(row[:, p, :], x1_d[bass.ds(b, 1), bass.ds(th * T + k * P, P), :]
                                    .rearrange("o p d -> p (o d)")).then_inc(row_loaded[p], 16)
                    rows(e, back_rows)

                    with e.Fori(0, NQ) as q:
                        e.wait_ge(w3_done, 1 + TB * (NQ * c + q))
                        settle(e)
                        e.dma_start(w3q[:], w3T[:, bass.ds(q * QD, QD)].rearrange("(k p) e -> p k e", p=P)) \
                            .then_inc(w3_loaded, 16)
                        e.wait_ge(out_stored, 1 + 16 * (NQ * c + q))
                        settle(e)
                        e.dma_start(res[:], x1_d[bass.ds(b, 1), bass.ds(th * T, T), bass.ds(q * QD, QD)]
                                    .rearrange("o (k p) e -> p (o k) e", p=P)).then_inc(res_loaded, 16)
            e.wait_ge(out_stored, 1 + 16 * NB * TH * NQ)
            settle(e)

        @block.gpsimd
        def _(pool):
            e = pool
            e.memset(ident[:], 0.0).then_inc(ident_step, 1)
            e.wait_ge(ident_step, 2)
            e.affine_select(out=ident[:], in_=ident[:], compare_op=ALU.not_equal, fill=1.0, base=0,
                            pattern=[[-1, P]], channel_multiplier=1).then_inc(ident_step, 1)
            e.wait_ge(masks, 4)
            e.wait_ge(ln1_step, 1 + NB * J + 1)
            e.tensor_tensor(r1[:], r1[:], half[:, 0:1].broadcast_to([P, NB * J]), ALU.pow).then_inc(rs_done, 1)
            with e.Fori(0, NB) as b:
                with e.Fori(0, TH) as th:
                    c = TH * b + th
                    e.wait_ge(bc_loaded, 1 + 32 * (c + 1))

                    def scan(j, j2, p):
                        g = J * c + 2 * j2 + p
                        for q in range(PAIRS):
                            s = 2 * (q % 2)
                            e.wait_ge(h_done, 1 + N * g + 2 * q + 3)
                            e.wait_ge(prod_summed, 1 + PAIRS * g + q)
                            e.tensor_tensor(prod[:, s:s + 2, :], h[:, s:s + 2, :], Cb[:, 2 * q:2 * q + 2, :],
                                            ALU.mult).then_inc(prod_done, 1)
                        e.wait_ge(xt_loaded, 1 + 16 * (g + 1))
                        e.wait_ge(yg_done, 1 + g + 1)
                        e.tensor_tensor(yg[:, p], yg[:, p], xt[:], ALU.add).then_inc(x1_done, 1)
                    steps(e, scan)

                    def rstd(k, k2, p):
                        f = TB * c + 2 * k2 + p
                        e.wait_ge(mv_step, 1 + 4 * f + 4)
                        e.tensor_tensor(r2[:, bass.ds(TB * th + k, 1)], mv[:, p, 1:2], half[:, 0:1], ALU.pow) \
                            .then_inc(rs_done, 1)
                    rows(e, rstd)
                with e.Fori(0, TH) as th:
                    c = TH * b + th

                    with e.Fori(0, NQ) as q:
                        e.wait_ge(res_loaded, 1 + 16 * (NQ * c + q + 1))
                        e.tensor_tensor(res[:], res[:],
                                        b3r[:, bass.ds(q * QD, QD)].unsqueeze(1).broadcast_to([P, TB, QD]),
                                        ALU.add).then_inc(rowb_done, 1)

        @block.tensor
        def _(pe):
            e = pe
            e.wait_ge(ident_step, 3)
            e.wait_ge(const_loaded, 1 + 16 * CONSTS)
            e.wait_ge(masks, 4)
            settle(e)
            with e.Fori(0, NB) as b:
                with e.Fori(0, TH) as th:
                    c = TH * b + th
                    e.wait_ge(ctx_loaded, 1 + 16 * (c + 1))

                    def in_proj(j, j2, p):
                        e.wait_ge(win_loaded[p], 1 + 16 * ((J // 2) * c + j2 + 1))
                        e.wait_ge(evac[p], 1 + front(p, b, th) + j2)
                        for k in range(DK):
                            mm = e.matmul(dense[:, p, :], win[:, p, k, :], ctxs[:, k, :],
                                          start=(k == 0), stop=(k == DK - 1))
                        mm.then_inc(xin_done, 1)
                    steps(e, in_proj)

                    e.wait_ge(u_done, 1 + J * (c + 1))
                    e.wait_ge(evac[0], 1 + front(0, b, th) + P1_E[0])
                    for k in range(J):
                        mm = e.matmul(dense[0:DR + 2 * N, 0, :], xpw[:, k, :], u[:, k, :],
                                      start=(k == 0), stop=(k == J - 1))
                    mm.then_inc(xdbl_done, 1)

                    def scan(j, j2, p):
                        g = J * c + 2 * j2 + p
                        at = [front(s, b, th) + P1_E[s] + P2_E[s] + 2 * j2 + p for s in (0, 1)]
                        e.wait_ge(dtrows_done, 1 + c + 1)
                        e.wait_ge(dtw_done, 1 + g + 1)
                        e.wait_ge(evac[p], 1 + at[p])
                        e.matmul(dense[:, p, :], dtw[:, p, :], dtaug[:], start=True, stop=True).then_inc(v_done, 1)
                        e.wait_ge(zn_done, 1 + g + 1)
                        e.wait_ge(evac[1 - p], 1 + at[1 - p])
                        for k in range(TB):
                            mm = e.transpose(dense[:, 1 - p, k * P:(k + 1) * P], xz[:, k * P:(k + 1) * P], ident[:])
                        mm.then_inc(zT_done, 1)
                        e.wait_ge(yg_done, 1 + g)
                        e.wait_ge(Du_done, 1 + g + 1)
                        for k in range(TB):
                            mm = e.matmul(yT[:, k, :], Du[:, k * P:(k + 1) * P], ident[:], is_transpose=True,
                                          start=(k == 0), stop=False, skip_group_check=True)
                        for q in range(PAIRS):
                            e.wait_ge(prod_done, 1 + PAIRS * g + q + 2)
                            for i in (0, 1):
                                for k in range(TB):
                                    mm = e.matmul(yT[:, k, :], prod[:, 2 * (q % 2) + i, k * P:(k + 1) * P], ident[:],
                                                  is_transpose=True, start=False,
                                                  stop=(q == PAIRS - 1 and i == 1), skip_group_check=True)
                            mm.then_inc(prod_summed, 1)
                    steps(e, scan)

                    def logits(k, k2, p):
                        f = TB * c + 2 * k2 + p
                        e.wait_ge(xn_done, 1 + 2 * TH * TB * b + TB * th + 2 * k2 + p + 2)
                        e.wait_ge(evac[p], 1 + front(p, b, th) + P1_E[p] + P2_E[p] + S_E[p] + k2)
                        for q in range(DI // SD):
                            e.wait_ge(sww_loaded[q % 2], 1 + 16 * (f * (DI // SD // 2) + q // 2 + 1))
                            for i in range(SD // 32):
                                mm = e.matmul(dense[32 * i:32 * i + 32, p, 0:32 * E],
                                              xn[:, q * SD + 32 * i:q * SD + 32 * i + 32],
                                              sww[:, q % 2, :, 32 * i:32 * i + 32],
                                              start=(q == 0), stop=(q == DI // SD - 1))
                            mm.then_inc(sw_used, 1)
                    rows(e, logits)

                e.wait_ge(lgr_done, 1 + TH * TB * (b + 1))
                e.wait_ge(evac[1], 1 + TH * TH_E[1] + b * B_E[1])
                for k in range(TH * TB):
                    mm = e.matmul(dense[:, 1, 0:E], ones[:], lgr[:, k, :], start=(k == 0), stop=(k == TH * TB - 1))
                mm.then_inc(lg_done, 1)

                with e.Fori(0, TH) as th:
                    c = TH * b + th

                    def turn(k, k2, p):
                        r = 2 * TH * TB * b + TB * (TH + th) + 2 * k2 + p
                        e.wait_ge(xn_done, 1 + r + 2)
                        for s in (0, 1):
                            e.wait_ge(evac[s], 1 + back(s, b, th) + 2 * k2 + p)
                            for i in range(J // 2):
                                d = (J // 2) * s + i
                                mm = e.transpose(dense[:, s, i * P:(i + 1) * P], xn[:, d * P:(d + 1) * P], ident[:])
                            mm.then_inc(tr_done, 1)
                    rows(e, turn)

                    e.wait_ge(sel_step, 1 + 9 * (b + 1))
                    for s in (0, 1):
                        e.wait_ge(evac[s], 1 + back(s, b, th) + F3T_E[s])
                        settle(e)
                    with e.Fori(0, J) as hp:
                        for i in (0, 1):
                            e.wait_ge(evac[i], 1 + back(i, b, th) + F3T_E[i] + (2 - i) * hp)
                            e.matmul(dense[:, i, :], w1s[:, i, :], xT[:, bass.ds(hp, 1), :].rearrange("p o t -> p (o t)"),
                                     start=True, stop=True).then_inc(hid_done, 1)
                        for i in (0, 1):
                            e.wait_ge(evac[i], 1 + back(i, b, th) + F3T_E[i] + (2 - i) * hp + 1)
                        for i in (0, 1):
                            mm = e.matmul(dense[:, 0, :], w2s[:, i, :], hs[:, i, :], start=(i == 0), stop=(i == 1))
                        mm.then_inc(o_done, 1)

                    e.wait_ge(evac[0], 1 + back(0, b, th) + F3T_E[0] + F3E_E[0])

                    settle(e)
                    with e.Fori(0, NQ) as q:
                        e.wait_ge(w3_loaded, 1 + 16 * (NQ * c + q + 1))
                        for k in range(TB):
                            s = k % 2
                            e.wait_ge(evac[s], 1 + back(s, b, th) + F3T_E[s] + F3E_E[s] + (TB // 2) * q + k // 2)
                            for d in range(J):
                                mm = e.matmul(dense[:, s, 0:QD], xT[:, d, k * P:(k + 1) * P], w3q[:, d, :],
                                              start=(d == 0), stop=(d == J - 1))
                            mm.then_inc(w3_done, 1)

        @block.scalar
        def _(act):
            e = act
            e.wait_ge(const_loaded, 1 + 16 * CONSTS)
            e.activation(Av[:], Av[:], ACT.Exp).then_inc(a_ready, 1)
            e.wait_ge(a_ready, 3)
            settle(e)
            with e.Fori(0, NB) as b:
                with e.Fori(0, TH) as th:
                    c = TH * b + th

                    def in_proj(j, j2, p):
                        g = J * c + 2 * j2 + p
                        e.wait_ge(conv_step, 1 + 6 * g)
                        e.wait_ge(bc_stored, 1 + 16 * c)
                        e.wait_ge(xin_done, 1 + g + 2)
                        e.copy(xpad[:, DC - 1:CH], dense[:, p, :]).then_inc(evac[p], 1)
                        e.wait_ge(conv_step, 1 + 6 * g + 5)
                        e.wait_ge(du_done, 1 + J * c)
                        e.wait_ge(Du_done, 1 + J * c)
                        e.wait_ge(xdbl_done, 1 + c)
                        e.activation(u[:, bass.ds(j, 1), :].rearrange("p o t -> p (o t)"), cacc[:], ACT.Silu) \
                            .then_inc(u_done, 1)
                    steps(e, in_proj)

                    e.wait_ge(xdbl_done, 1 + c + 1)
                    e.wait_ge(v_done, 1 + J * c + 1)
                    e.copy(dtaug[0:DR, :], dense[0:DR, 0, :]).then_inc(dtrows_done, 1)
                    e.wait_ge(bc_stored, 1 + 16 * c)
                    e.copy(bcs, dense[DR:DR + 2 * N, 0, :]).then_inc(evac[0], 1)

                    def scan(j, j2, p):
                        g = J * c + 2 * j2 + p
                        at = front(p, b, th) + P1_E[p] + P2_E[p] + 2 * j2 + p
                        e.wait_ge(v_done, 1 + g)
                        e.copy(dtw[:, p, :], dtall[:, bass.ds(j * P, P)]).then_inc(dtw_done, 1)
                        e.wait_ge(nm_done, 2)
                        e.wait_ge(xz_loaded, 1 + 16 * (g + 1))
                        e.activation(xz[:], xz[:], ACT.Identity, scale=r1[:, bass.ds(J * b + 2 * j2 + p, 1)],
                                     bias=nm1[:, bass.ds(J * b + 2 * j2 + p, 1)]).then_inc(zn_done, 1)
                        e.wait_ge(v_done, 1 + g + 2)
                        e.wait_ge(evac[p], 1 + at)
                        e.activation(sp[:], dense[:, p, :], ACT.Abs).then_inc(sp_step, 1)
                        e.wait_ge(sp_step, 1 + 3 * g + 1)
                        e.activation(sp[:], sp[:], ACT.Exp, scale=-1.0).then_inc(sp_step, 1)
                        e.wait_ge(sp_step, 1 + 3 * g + 2)
                        e.activation(sp[:], sp[:], ACT.Ln, bias=1.0).then_inc(sp_step, 1)
                        e.wait_ge(prod_summed, 1 + PAIRS * g + 1)
                        e.activation(Du[:], u[:, bass.ds(j, 1), :].rearrange("p o t -> p (o t)"), ACT.Copy,
                                     scale=Dv[:, bass.ds(j, 1)]).then_inc(Du_done, 1)
                        e.wait_ge(zT_done, 1 + g + 1)
                        e.wait_ge(yg_done, 1 + g)
                        e.activation(szT[:].rearrange("p k e -> p (k e)"), dense[:, 1 - p, :], ACT.Silu) \
                            .then_inc(evac[1 - p], 1)
                        e.wait_ge(evac[p], 1 + at + 1)
                        for n in range(N):
                            e.wait_ge(h_done, 1 + N * g + n)
                            e.activation(dA[:, n % 2, :], delta[:, p, :], ACT.Exp,
                                         scale=Av[:, bass.ds(j * N + n, 1)]).then_inc(dA_done, 1)
                    steps(e, scan)

                    def norm(k, k2, p):
                        f = TB * c + 2 * k2 + p
                        r = 2 * TH * TB * b + TB * th + 2 * k2 + p
                        e.wait_ge(nm_done, 1 + f + 2)
                        e.wait_ge(row_loaded[p], 1 + 16 * (NB * J // 2 + TH * TB * b + (TB // 2) * th + k2 + 1))
                        e.wait_ge(sw_used, 1 + (DI // SD) * f + 1)
                        e.wait_ge(tr_done, 1 + 2 * TB * TH * b)
                        e.activation(xn[:], row[:, p, :], ACT.Identity, scale=r2[:, bass.ds(TB * th + k, 1)],
                                     bias=nm2[:, bass.ds(TB * th + k, 1)]).then_inc(xn_done, 1)
                    rows(e, norm)

                e.wait_ge(route_step, 1 + 5 * b + 2)
                e.activation(rt[:, 1, :], rt[:, 0, :], ACT.Exp, bias=rt[:, 7, 0:1], accum_out=rt[:, 7, 1:2]) \
                    .then_inc(pexp_done, 1)

                with e.Fori(0, TH) as th:
                    c = TH * b + th

                    def norm_again(k, k2, p):
                        r = 2 * TH * TB * b + TB * (TH + th) + 2 * k2 + p
                        e.wait_ge(row_loaded[p], 1 + 16 * (NB * J // 2 + TH * TB * b + (TB // 2) * (TH + th) + k2 + 1))
                        e.wait_ge(tr_done, 1 + 2 * (TB * c + 2 * k2 + p))
                        e.wait_ge(sw_used, 1 + (DI // SD) * TB * TH * (b + 1) + 1)
                        e.wait_ge(sel_step, 1 + 9 * (b + 1))
                        e.activation(xn[:], row[:, p, :], ACT.Identity, scale=r2[:, bass.ds(TB * th + k, 1)],
                                     bias=nm2[:, bass.ds(TB * th + k, 1)]).then_inc(xn_done, 1)
                        for s in (0, 1):
                            e.wait_ge(tr_done, 1 + 2 * (TB * c + 2 * k2 + p) + s + 1)
                            e.wait_ge(w3_done, 1 + NQ * TB * c)
                            e.copy(xT[:, (J // 2) * s:(J // 2) * (s + 1), bass.ds(k * P, P)],
                                   dense[:, s, :].rearrange("p (d t) -> p d t", t=P)).then_inc(evac[s], 1)
                    rows(e, norm_again)

                    with e.Fori(0, J) as hp:
                        for i in (0, 1):
                            e.wait_ge(hid_done, 1 + 2 * J * c + 2 * hp + i + 1)
                            e.wait_ge(o_done, 1 + J * c + hp)
                            e.wait_ge(sel_step, 1 + 9 * (b + 1))
                            e.activation(hs[:, i, :], dense[:, i, :], ACT.Gelu, bias=b1s[:, i:i + 1]) \
                                .then_inc(evac[i], 1)
                    with e.Fori(0, NQ) as q:
                        for s in (0, 1):
                            e.wait_ge(evac[s], 1 + back(s, b, th) + F3T_E[s] + F3E_E[s] + (TB // 2) * (q + 1))
                        e.dma_start(out[bass.ds(b, 1), bass.ds(th * T, T), bass.ds(q * QD, QD)]
                                    .rearrange("o (k p) e -> p (o k) e", p=P), res[:]).then_inc(out_stored, 16)

        @block.vector
        def _(dve):
            e = dve
            e.memset(ones[:], 1.0).then_inc(masks, 1)
            e.memset(half[:], -0.5).then_inc(masks, 1)
            e.memset(dtaug[DR:DR + 1, :], 1.0).then_inc(masks, 1)
            for i in range(E):
                e.memset(iota[:, i:i + 1], float(i)).then_inc(set_up, 1)
            e.memset(w1s[:], 0.0).then_inc(set_up, 1)
            e.memset(w2s[:], 0.0).then_inc(set_up, 1)
            e.wait_ge(ident_step, 3)
            e.wait_ge(set_up, 1 + E + 2)
            e.tensor_copy(diag[:], ident[:, 0:32]).then_inc(set_up, 1)
            for i in range(1, 4):
                e.wait_ge(set_up, 1 + E + 2 + i)
                e.tensor_tensor(diag[:], diag[:], ident[:, 32 * i:32 * i + 32], ALU.add).then_inc(set_up, 1)
            e.wait_ge(a_ready, 2)
            e.tensor_scalar(Av[:], Av[:], -1.0, None, ALU.mult).then_inc(a_ready, 1)
            with e.Fori(0, NB * J // 2) as i2:
                for p in (0, 1):
                    e.wait_ge(row_loaded[p], 1 + 16 * (i2 + 1))
                    e.wait_ge(ln1_step, 1 + 2 * i2 + p)
                    for i in (0, 1):
                        bn = e.bn_stats(bst[:, p, i, :], row[:, p, i * T:(i + 1) * T])
                        if i == 0:
                            bn.then_inc(bn_step, 1)
                    bn.then_inc(row_read, 1)
                    e.wait_ge(bn_step, 1 + 2 * i2 + p + 1)
                    e.wait_ge(row_read, 1 + 2 * i2 + p + 2)
                    settle(e)
                    e.bn_aggr(mv[:, p, :], bst[:, p].rearrange("p a b -> p (a b)")).then_inc(mv1_step, 1)
                    e.wait_ge(mv1_step, 1 + 2 * i2 + p + 1)
                    settle(e)
                    e.tensor_copy(mv1[:, bass.ds(2 * i2 + p, 1), :], mv[:, p, :].unsqueeze(1)).then_inc(ln1_step, 1)
            e.wait_ge(ln1_step, 1 + NB * J)
            e.tensor_scalar(r1[:], mv1[:, :, 1], EPS, None, ALU.add).then_inc(ln1_step, 1)
            e.wait_ge(rs_done, 2)
            e.scalar_tensor_tensor(out=nm1[:], in0=mv1[:, :, 0], scalar=-1.0, in1=r1[:], op0=ALU.mult, op1=ALU.mult) \
                .then_inc(nm_done, 1)

            with e.Fori(0, NB) as b:
                e.memset(halo[:], 0.0).then_inc(zeroed, 1)
                e.memset(state[:], 0.0).then_inc(zeroed, 1)
                e.wait_ge(zeroed, 1 + 2 * b + 2)
                settle(e)
                with e.Fori(0, TH) as th:
                    c = TH * b + th

                    def conv(j, j2, p):
                        g = J * c + 2 * j2 + p
                        tail = halo[:, bass.ds(j, 1), :].rearrange("p o t -> p (o t)")

                        def tap(k):
                            return cw[:, bass.ds(j, 1), k:k + 1].rearrange("p o t -> p (o t)")
                        e.wait_ge(bc_stored, 1 + 16 * c)
                        e.tensor_copy(xpad[:, 0:DC - 1], tail).then_inc(conv_step, 1)
                        e.wait_ge(evac[p], 1 + front(p, b, th) + j2 + 1)
                        e.wait_ge(u_done, 1 + g)
                        e.tensor_scalar(cacc[:], xpad[:, DC - 1:CH], tap(DC - 1), cb[:, bass.ds(j, 1)],
                                        ALU.mult, ALU.add).then_inc(conv_step, 1)
                        for k in range(DC - 2, -1, -1):
                            e.wait_ge(conv_step, 1 + 6 * g + DC - k)
                            e.scalar_tensor_tensor(out=cacc[:], in0=xpad[:, k:k + T], scalar=tap(k), in1=cacc[:],
                                                   op0=ALU.mult, op1=ALU.add).then_inc(conv_step, 1)
                        e.tensor_copy(tail, xpad[:, T:CH]).then_inc(conv_step, 1)
                        e.wait_ge(conv_step, 1 + 6 * g + 6)
                    steps(e, conv)

                    e.wait_ge(bc_loaded, 1 + 32 * (c + 1))

                    def scan(j, j2, p):
                        g = J * c + 2 * j2 + p
                        e.wait_ge(sp_step, 1 + 3 * g + 3)
                        e.scalar_tensor_tensor(out=delta[:, p, :], in0=dense[:, p, :], scalar=0.0, in1=sp[:],
                                               op0=ALU.max, op1=ALU.add).then_inc(evac[p], 1)
                        e.wait_ge(evac[p], 1 + front(p, b, th) + P1_E[p] + P2_E[p] + 2 * j2 + p + 1)
                        e.tensor_tensor(du[:], delta[:, p, :], u[:, bass.ds(j, 1), :].rearrange("p o t -> p (o t)"),
                                        ALU.mult).then_inc(du_done, 1)
                        e.wait_ge(du_done, 1 + g + 1)

                        def times_b(q):
                            s = 2 * (q % 2)
                            e.tensor_tensor(duB[:, s:s + 2, :], du[:].unsqueeze(1).broadcast_to([P, 2, T]),
                                            Bb[:, 2 * q:2 * q + 2, :], ALU.mult).then_inc(duB_done, 1)

                        def keep(q):
                            s = 2 * (q % 2)
                            e.wait_ge(h_done, 1 + N * g + 2 * q + 3)
                            settle(e)
                            e.tensor_copy(state[:, bass.ds(j * N + 2 * q, 2)], h[:, s:s + 2, T - 1]).then_inc(saved, 1)

                        times_b(0)
                        for q in range(PAIRS):
                            if q + 1 < PAIRS:
                                if q >= 1:
                                    e.wait_ge(h_done, 1 + N * g + 2 * q + 1)
                                times_b(q + 1)
                            e.wait_ge(duB_done, 1 + PAIRS * g + q + 1)
                            e.wait_ge(prod_done, 1 + PAIRS * g + q)
                            e.wait_ge(saved, 1 + PAIRS * g + max(q - 1, 0))
                            for i in (0, 1):
                                n = 2 * q + i
                                e.wait_ge(dA_done, 1 + N * g + n + 1)
                                e.tensor_tensor_scan(h[:, n % 4, :], dA[:, n % 2, :], duB[:, n % 4, :],
                                                     state[:, bass.ds(j * N + n, 1)], ALU.mult, ALU.add) \
                                    .then_inc(h_done, 1)
                            if q >= 1:
                                keep(q - 1)
                        keep(PAIRS - 1)
                        e.wait_ge(saved, 1 + PAIRS * (g + 1))
                        e.wait_ge(prod_summed, 1 + PAIRS * (g + 1) + 1)
                        e.wait_ge(evac[1 - p], 1 + front(1 - p, b, th) + P1_E[1 - p] + P2_E[1 - p] + 2 * j2 + p + 1)
                        e.wait_ge(x1_stored[p], 1 + 16 * ((J // 2) * c + j2))
                        e.tensor_tensor(yg[:, p], yT[:], szT[:], ALU.mult).then_inc(yg_done, 1)
                    steps(e, scan)

                    def stats(k, k2, p):
                        f = TB * c + 2 * k2 + p
                        e.wait_ge(row_loaded[p], 1 + 16 * (NB * J // 2 + TH * TB * b + (TB // 2) * th + k2 + 1))
                        for i in (0, 1):
                            e.bn_stats(bst[:, p, i, :], row[:, p, i * T:(i + 1) * T]).then_inc(mv_step, 1)
                        e.wait_ge(mv_step, 1 + 4 * f + 2)
                        settle(e)
                        e.bn_aggr(mv[:, p, :], bst[:, p].rearrange("p a b -> p (a b)")).then_inc(mv_step, 1)
                        e.wait_ge(mv_step, 1 + 4 * f + 3)
                        e.tensor_scalar(mv[:, p, 1:2], mv[:, p, 1:2], EPS, None, ALU.add).then_inc(mv_step, 1)
                        e.wait_ge(rs_done, 1 + f + 2)
                        e.scalar_tensor_tensor(out=nm2[:, bass.ds(TB * th + k, 1)], in0=mv[:, p, 0:1], scalar=-1.0,
                                               in1=r2[:, bass.ds(TB * th + k, 1)], op0=ALU.mult, op1=ALU.mult) \
                            .then_inc(nm_done, 1)
                        e.wait_ge(sw_used, 1 + (DI // SD) * (f + 1) + 1)
                        e.tensor_tensor(lgm[:], dense[:, p, 0:32 * E].rearrange("p (e i) -> p e i", i=32),
                                        diag[:].unsqueeze(1).broadcast_to([P, E, 32]), ALU.mult).then_inc(evac[p], 1)
                        e.wait_ge(evac[p], 1 + front(p, b, th) + P1_E[p] + P2_E[p] + S_E[p] + k2 + 1)
                        e.wait_ge(lg_done, 1 + b)
                        e.tensor_reduce(lgr[:, bass.ds(TB * th + k, 1), :].rearrange("p o e -> p (o e)"), lgm[:],
                                        AX.X, ALU.add).then_inc(lgr_done, 1)
                        e.wait_ge(lgr_done, 1 + f + 1)
                    rows(e, stats)

                e.wait_ge(lg_done, 1 + b + 1)
                e.tensor_tensor(rt[:, 0, :], dense[:, 1, 0:E], swb[:], ALU.add).then_inc(evac[1], 1)
                e.wait_ge(evac[1], 1 + b * B_E[1] + TH * TH_E[1] + 1)
                settle(e)
                e.max(rt[:, 4, :], rt[:, 0, :]).then_inc(route_step, 1)
                e.wait_ge(route_step, 1 + 5 * b + 1)
                e.tensor_scalar(rt[:, 7, 0:1], rt[:, 4, 0:1], -1.0, None, ALU.mult).then_inc(route_step, 1)
                e.wait_ge(pexp_done, 1 + b + 1)
                e.reciprocal(rt[:, 7, 2:3], rt[:, 7, 1:2]).then_inc(route_step, 1)
                e.wait_ge(route_step, 1 + 5 * b + 3)
                e.tensor_scalar(rt[:, 2, :], rt[:, 1, :], rt[:, 7, 2:3], None, ALU.mult).then_inc(route_step, 1)
                e.wait_ge(route_step, 1 + 5 * b + 4)
                settle(e)
                e.max(rt[:, 3, :], rt[:, 2, :]).then_inc(route_step, 1)
                e.wait_ge(route_step, 1 + 5 * b + 5)
                settle(e)
                e.max_index(idx[:], rt[:, 3, :], rt[:, 2, :]).then_inc(top_step, 1)
                e.wait_ge(top_step, 1 + 4 * b + 1)
                e.tensor_copy(rt[:, 5, :], idx[:]).then_inc(top_step, 1)
                e.wait_ge(top_step, 1 + 4 * b + 2)
                for i in (0, 1):
                    e.tensor_scalar(hot[:, i, :], iota[:], rt[:, 5, i:i + 1], None, ALU.is_equal).then_inc(top_step, 1)
                e.wait_ge(top_step, 1 + 4 * b + 4)
                e.wait_ge(o_done, 1 + TH * J * b)
                e.wait_ge(experts_loaded, 1 + 64 * (b + 1))
                n = 0
                for i in (0, 1):
                    for src, dst in ((w12[:, 0], w1s), (w12[:, 1], w2s)):
                        e.wait_ge(wt_step, 1 + 8 * b + 2 * n)
                        e.wait_ge(sel_half, 1 + 4 * b + n)
                        e.tensor_tensor(wt, src, hot[:, i, :].unsqueeze(2).broadcast_to([P, E, HD]),
                                        ALU.mult).then_inc(wt_step, 1)
                        e.wait_ge(wt_step, 1 + 8 * b + 2 * n + 1)
                        for lo in (0, HD):
                            red = e.tensor_reduce(dst[lo:lo + HD, i, lo:lo + HD],
                                                  wt[lo:lo + HD].rearrange("p e f -> p f e"), AX.X, ALU.add)
                            if lo == 0:
                                red.then_inc(sel_half, 1)
                        red.then_inc(wt_step, 1)
                        n += 1
                    e.tensor_tensor_reduce(rt[:, 6, :], b1c[:], hot[:, i, :], 1.0, 0.0, ALU.mult, ALU.add,
                                           b1s[:, i:i + 1]).then_inc(sel_step, 1)
                    e.wait_ge(sel_step, 1 + 9 * b + 4 * i + 1)
                    e.tensor_tensor_reduce(rt[:, 6, :], b2c[:], hot[:, i, :], 1.0, 0.0, ALU.mult, ALU.add,
                                           b2s[:, i:i + 1]).then_inc(sel_step, 1)
                    e.wait_ge(sel_half, 1 + 4 * b + 2 * i + 2)
                    e.wait_ge(wt_step, 1 + 8 * b + 2 * n)
                    e.wait_ge(sel_step, 1 + 9 * b + 4 * i + 2)
                    e.tensor_scalar(w2s[:, i, :], w2s[:, i, :], rt[:, 3, i:i + 1], None, ALU.mult).then_inc(sel_step, 1)
                    e.tensor_scalar(b2s[:, i:i + 1], b2s[:, i:i + 1], rt[:, 3, i:i + 1], None, ALU.mult) \
                        .then_inc(sel_step, 1)
                    e.wait_ge(sel_step, 1 + 9 * b + 4 * i + 4)
                e.tensor_tensor(b2s[:, 2:3], b2s[:, 0:1], b2s[:, 1:2], ALU.add).then_inc(sel_step, 1)
                e.wait_ge(sel_step, 1 + 9 * (b + 1))

                settle(e)
                with e.Fori(0, TH) as th:
                    c = TH * b + th
                    for s in (0, 1):
                        e.wait_ge(evac[s], 1 + back(s, b, th) + F3T_E[s])
                        settle(e)
                    with e.Fori(0, J) as hp:
                        part = xT[:, bass.ds(hp, 1), :].rearrange("p o t -> p (o t)")
                        e.wait_ge(o_done, 1 + J * c + hp + 1)
                        e.wait_ge(evac[0], 1 + back(0, b, th) + F3T_E[0] + 2 * hp + 1)
                        e.scalar_tensor_tensor(out=part, in0=dense[:, 0, :], scalar=b2s[:, 2:3], in1=part,
                                               op0=ALU.add, op1=ALU.add).then_inc(evac[0], 1)

                    with e.Fori(0, NQ) as q:
                        e.wait_ge(rowb_done, 1 + NQ * c + q + 1)
                        for k in range(TB):
                            e.wait_ge(w3_done, 1 + TB * (NQ * c + q) + k + 1)
                            e.tensor_tensor(res[:, k, :], dense[:, k % 2, 0:QD], res[:, k, :], ALU.add) \
                                .then_inc(evac[k % 2], 1)


def kernel(**inputs):
    import numpy as _np
    import concourse.bacc as _bacc
    from concourse import mybir as _mybir
    from concourse.bass_utils import run_bass_kernel_spmd as _run

    def get(name):
        return _np.asarray(inputs[name])

    laid = {
        "x": get("x"),
        "ctxT": get("ctx_1024").transpose(0, 2, 1),
        "w_inT": get("L0_xattn_in_proj_w").T,
        "conv_w": get("L0_xattn_conv_w"),
        "conv_b": get("L0_xattn_conv_b"),
        "x_projT": get("L0_xattn_x_proj_w").T,
        "dt_projT": get("L0_xattn_dt_proj_w").T,
        "dt_b": get("L0_xattn_dt_proj_b").reshape(1, -1),
        "A_log": get("L0_xattn_A_log"),
        "D": get("L0_xattn_D"),
        "sw": get("L0_ffn_switch_w").reshape(E, L, DI),
        "sw_b": get("L0_ffn_switch_b"),
        "w1T": get("L0_ffn_w1").transpose(0, 2, 1),
        "b1": get("L0_ffn_b1"),
        "w2T": get("L0_ffn_w2").transpose(0, 2, 1),
        "b2": get("L0_ffn_b2"),
        "w3T": get("L0_ffn_w3").T,
        "b3": get("L0_ffn_b3"),
    }
    nc = _bacc.Bacc("TRN2", target_bir_lowering=False, num_devices=1)
    arrays, args = {}, []
    for name, a in laid.items():
        a = _np.ascontiguousarray(a)
        arrays[f"in_{name}"] = a
        args.append(nc.dram_tensor(f"in_{name}", a.shape, _mybir.dt.from_np(a.dtype), kind="ExternalInput").ap())
    args.append(nc.dram_tensor("out_0", (NB, L, DI), _mybir.dt.float32, kind="ExternalOutput").ap())
    build(nc, *args)
    r = _run(nc, [arrays], core_ids=[0])
    return r.results[0]["out_0"]
```

```python
from contextlib import ExitStack

import concourse.bass as bass
from concourse import mybir

F32 = mybir.dt.float32
U32 = mybir.dt.uint32
ALU = mybir.AluOpType
ACT = mybir.ActivationFunctionType
AX = mybir.AxisListType

P = 128
NB, L, DI, DM = 4, 1024, 1024, 512
T = 512
TH = L // T
TB = T // P
J = DI // P
N = 16
DR = 32
DC = 4
E = 8
HD = 64
DK = DM // P
EPS = 1e-5
PAIRS = N // 2
CH = T + DC - 1
SD = 128
QD = 256
NQ = DI // QD
B3 = 64
RA = 2
SLOTS = PAIRS
STEPS = TH * J
AHEAD = 10
UR = 2 * J
NT = NQ * TB
S, F0, F1 = 0, 1, 2


class Plan:

    def __init__(self, scan, old):
        self.scan, self.old = scan, old
        self.slots = [[] for _ in range(STEPS * SLOTS)]
        rows = []
        if scan:
            for st in range(STEPS):
                t = SLOTS * st
                self.add(t, "in_proj", st)
                if st % J == J - 2:
                    self.add(t + 1, "x_proj", st // J)
                self.add(t + 3, "zT", st)
                self.add(t + 4, "v", st)
            for k in range(J):
                rows.append((36 + 4 * k, "ln1", k))
                self.add(39 + 4 * k, "ln1_stats", k)
            self.add(122, "ln1_rstd")
            self.add(124, "ln1_shift")
        if old:
            for k in range(TB):
                self.logits(TB + k, 4 + 5 * k, 4, rows, F0 + k % 2)
            self.add(29, "logit_sum")
            self.add(30, "route")
            for u, turned, hidden, tiles in (
                (0, [30, 32, 34, 36], 37, [53 + 24 * i // NT for i in range(NT)]),
                (1, [77, 79, 81, 83], 85, [101 + 25 * i // NT for i in range(NT)]),
            ):
                for k in range(TB):
                    rows.append((turned[k] - 3, "turn", u, k))
                    self.add(turned[k] - 1, "renorm", u, k)
                    self.add(turned[k], "turn", u, k)
                for hp in range(J):
                    self.add(hidden + 2 * hp, "hidden", u, hp)
                    self.add(hidden + 2 * hp + 1, "expert_out", u, hp)
                for i in range(NT):
                    if i % TB == 0:
                        self.add(tiles[i - 1] if i else hidden, "w3_load", u, i // TB)
                    self.add(max(tiles[i] - 4, hidden), "res_load", u, i)
                    self.add(tiles[i], "tile", u, i)
                    self.add(tiles[i] + 1, "tile_out", u, i)
        if scan:
            for k in range(TB):
                self.logits(k, 96 + 6 * k, 5, rows, F1)
        self.row = {}
        for i, (t, *what) in enumerate(sorted(rows, key=lambda r: r[0])):
            self.row[tuple(what)] = i
            self.slots[t].insert(0, ("row_load", *what))
        self.rows = len(rows)
        self.table = {}
        for t, slot in enumerate(self.slots):
            after = [("silu", t)] if scan and t % SLOTS == 4 else []
            after += [("gelu", t) for what, *_ in slot if scan and what == "hidden"]
            for name in after:
                self.table[name] = len(self.table)
        self.use, self.uses = {}, [0, 0, 0]
        for slot in self.slots:
            for what, *args in slot:
                for name, bank in self.banks(what, args):
                    self.use[name] = (bank, self.uses[bank])
                    self.uses[bank] += 1

    def add(self, t, *what):
        self.slots[t].append(what)

    def logits(self, k, t, span, rows, bank):
        rows.append((t, "logits", k))
        self.add(t + 2, "stats", k)
        self.add(t + 2, "rstd", k)
        self.add(t + 4, "shift", k)
        self.add(t + 4, "norm", k)
        loads = DI // SD
        for i in range(loads):
            at = t + 5 + i * span // loads
            self.add(at - 2, "sw_load", k, i)
            self.add(at, "logit", k, i, bank)
        self.add(t + 5 + span, "diagonal", k)

    @staticmethod
    def banks(what, args):
        if what in ("in_proj", "x_proj", "zT", "v"):
            return [((what, *args), S)]
        if what == "logit" and args[1] == 0:
            return [(("logit", args[0]), args[2])]
        if what == "logit_sum":
            return [(("logit_sum",), F0)]
        if what in ("turn", "hidden"):
            return [((what, *args, 0), F0), ((what, *args, 1), F1)]
        if what == "expert_out":
            return [((what, *args), F0)]
        if what == "tile":
            return [((what, *args), F1 if args[0] == 0 and args[1] % 2 else F0)]
        return []


FIRST, NEXT, LAST = Plan(True, False), Plan(True, True), Plan(False, True)
LEAD_USES = (AHEAD // 2 + 2, AHEAD // 2, 0)


def build(nc, x, ctxT, w_inT, conv_w, conv_b, x_projT, dt_projT, dt_b, A_log, D, sw, sw_b,
          w1T, b1, w2T, b2, w3T, b3, out):
    x1_d = nc.dram_tensor("x1_scratch", (NB, L, DI), F32, kind="Internal").ap()
    bc_d = nc.dram_tensor("bc_scratch", (NB * TH + 1, 2 * N, T), F32, kind="Internal").ap()

    with ExitStack() as ctx:
        def sb(name, shape, dt=F32):
            return ctx.enter_context(nc.sbuf_tensor(name, shape, dt))

        counts = []

        def sem(name, start=0):
            s = ctx.enter_context(nc.semaphore(name))
            counts.append((s, 1 + start))
            return s

        ident = sb("ident", [P, P])
        ones = sb("ones", [P, P])
        diag = sb("diag", [P, 32])
        iota = sb("iota", [P, E])
        half = sb("half", [P, 3])
        xpw = sb("xpw", [P, J, DR + 2 * N])
        dtw = sb("dtw", [B3 + 1, DI])
        cw = sb("cw", [P, J, DC])
        cb = sb("cb", [P, J])
        Dv = sb("Dv", [P, J])
        Av = sb("Av", [P, J * N])
        b1c = sb("b1c", [P, E])
        b2c = sb("b2c", [P, E])
        swb = sb("swb", [P, E])
        ctxs = sb("ctxs", [P, DK, T])
        win = sb("win", [P, 2, DK, P])
        xpad = sb("xpad", [P, CH])
        halo = sb("halo", [P, J, DC - 1])
        cacc = sb("cacc", [P, T])
        u = sb("u", [P, UR, T])
        dtaug = sb("dtaug", [DR + 1, TH, T])
        Bb = sb("Bb", [P, N, T])
        Cb = sb("Cb", [P, N, T])
        sp = sb("sp", [P, T])
        delta = sb("delta", [P, 2, T])
        dA = sb("dA", [P, RA, T])
        h = sb("h", [P, 4, T])
        prod = sb("prod", [P, 4, T])
        state = sb("state", [P, J * N])
        Dd = sb("Dd", [P, P])
        xz = sb("xz", [P, T])
        szT = sb("szT", [P, TB, P])
        xt = sb("xt", [P, TB, P])
        mv1 = sb("mv1", [P, J, 2])
        r1 = sb("r1", [P, J])
        nm1 = sb("nm1", [P, J])
        row = sb("row", [P, 2, DI])
        bst = sb("bst", [P, 2, 6])
        mv = sb("mv", [P, 2])
        r2 = sb("r2", [P, 2 * TB])
        nm2 = sb("nm2", [P, 2 * TB])
        sww = sb("sww", [P, 2, E, SD])
        lgm = sb("lgm", [P, E, 32])
        lgr = sb("lgr", [P, 2 * TB, E])
        rt = sb("rt", [P, 7, E])
        idx = sb("idx", [P, E], U32)
        hot = sb("hot", [P, 4, E])
        w1s = sb("w1s", [P, 2, HD])
        w2s = sb("w2s", [P, HD])
        b1s = sb("b1s", [P, 1])
        b2s = sb("b2s", [P, 1])
        xT = sb("xT", [P, J, T])
        hs = sb("hs", [P, 2, T])
        w3q = sb("w3q", [P, J, QD])
        res = sb("res", [P, TB, QD])
        bcs = sp[DR:DR + 2 * N, :]
        w12 = hs[:].rearrange("p i (e f) -> p i e f", e=E)
        wt = sww[:, 0].rearrange("p e s -> p (e s)")[:, 0:E * HD].rearrange("p (e f) -> p e f", e=E)

        duB = ctx.enter_context(nc.psum_tensor("duB", [P, 3, T], F32))
        du = ctx.enter_context(nc.psum_tensor("du", [P, T], F32))
        yT = ctx.enter_context(nc.psum_tensor("yT", [P, TB, P], F32))
        dense = ctx.enter_context(nc.psum_tensor("dense", [P, 3, T], F32))

        const_loaded = sem("const_loaded")
        ctx_loaded = sem("ctx_loaded")
        win_loaded = [sem(f"win_loaded{p}") for p in (0, 1)]
        bc_stored = sem("bc_stored")
        bc_loaded = [sem(f"bc_loaded{q}") for q in range(PAIRS)]
        xz_loaded = sem("xz_loaded")
        xt_loaded = sem("xt_loaded")
        x1_stored = sem("x1_stored")
        row_loaded = [sem(f"row_loaded{p}") for p in (0, 1)]
        sww_loaded = [sem(f"sww_loaded{p}") for p in (0, 1)]
        experts_loaded = sem("experts_loaded")
        w3_loaded = sem("w3_loaded")
        res_loaded = [sem(f"res_loaded{k}") for k in range(TB)]
        out_stored = [sem(f"out_stored{k}") for k in range(TB)]
        set_up = sem("set_up")
        ident_step = sem("ident_step")
        masks = sem("masks")
        a_ready = sem("a_ready")
        evac = [sem(f"evac{s}") for s in range(3)]
        xin_done = sem("xin_done", start=1)
        conv_step = sem("conv_step")
        u_done = sem("u_done")
        xdbl_done = sem("xdbl_done")
        dtrows_done = sem("dtrows_done")
        v_done = sem("v_done")
        sp_step = sem("sp_step")
        du_done = sem("du_done")
        dA_done = sem("dA_done")
        duB_done = sem("duB_done")
        h_done = sem("h_done", start=RA - 1)
        saved = sem("saved")
        prod_done = sem("prod_done", start=1)
        prod_summed = sem("prod_summed", start=PAIRS)
        Dd_done = sem("Dd_done")
        zn_done = sem("zn_done")
        zT_done = sem("zT_done")
        yg_done = sem("yg_done")
        x1_done = sem("x1_done")
        ln1_step = sem("ln1_step")
        ln1_rs = sem("ln1_rs")
        ln1_done = sem("ln1_done")
        row_free = [sem(f"row_free{p}") for p in (0, 1)]
        mv_step = sem("mv_step")
        rs_done = sem("rs_done")
        nm_done = sem("nm_done")
        norm_done = sem("norm_done")
        sw_used = sem("sw_used", start=1)
        lgr_done = sem("lgr_done")
        lg_done = sem("lg_done")
        route_step = sem("route_step")
        pexp_done = sem("pexp_done")
        top_step = sem("top_step")
        sel_step = sem("sel_step")
        renorm_done = sem("renorm_done")
        tr_done = sem("tr_done")
        hid_done = sem("hid_done")
        o_done = sem("o_done")
        w3_done = sem("w3_done")
        table_step = sem("table_step")
        settled = sem("settled")

        CONSTS = 13
        MASKS = 4
        for s_, start in counts:
            nc.sync.sem_inc(s_, start)
        nc.all_engine_barrier()
        block = ctx.enter_context(nc.Block())

        def settle(eng):
            eng.sem_inc(settled, 1)

        def turns(eng, slot):
            for t in range(STEPS * SLOTS):
                slot(0, FIRST, t)
            with eng.Fori(1, NB) as b:
                for t in range(STEPS * SLOTS):
                    slot(b, NEXT, t)
            for t in range(STEPS * SLOTS):
                slot(NB, LAST, t)

        def count(plan, b, name):
            bank, at = plan.use[name]
            if plan is FIRST:
                return LEAD_USES[bank] + at
            return NEXT.uses[bank] * (b - 1) + (LEAD_USES[bank] + FIRST.uses[bank] + at)

        def bank_of(plan, name):
            return plan.use[name][0]

        def row_at(plan, b, what):
            i = plan.row[what]
            if plan is FIRST:
                return i % 2, J // 2 + i // 2
            return i % 2, NEXT.rows // 2 * (b - 1) + (J // 2 + FIRST.rows // 2 + i // 2)

        def late(plan, t, q):
            return t % SLOTS == q and (t >= SLOTS or plan is not FIRST) and (plan.scan or t < SLOTS)

        def chunk_block(G):
            return G // STEPS, G // J % TH, G % J

        def wrap(b):
            return b % NB

        def f_index(b, k):
            return 2 * TB * b + k

        def logit_batch(b, k):
            return b - 1 if k >= TB else b

        @block.sync
        def _(sync):
            e = sync

            def load_row(p, src):
                e.dma_start(row[:, p, :], src.rearrange("o p d -> p (o d)")).then_inc(row_loaded[p], 16)

            def load_win(G, j):
                e.dma_start(win[:, G % 2], w_inT[:, j * P:(j + 1) * P].rearrange("(k p) e -> p k e", p=P)) \
                    .then_inc(win_loaded[G % 2], 16)

            def load_ctx(b, th):
                e.dma_start(ctxs[:], ctxT[bass.ds(b, 1), :, th * T:(th + 1) * T]
                            .rearrange("o (k p) t -> p (o k) t", p=P)).then_inc(ctx_loaded, 16)

            def load_bc(c, q):
                for i, dst in ((0, Bb), (N, Cb)):
                    e.dma_start(dst[:, 2 * q:2 * q + 2, :], bc_d[bass.ds(c, 1), i + 2 * q:i + 2 * q + 2, :]
                                .rearrange("o n t -> (o n) t").partition_broadcast(P)).then_inc(bc_loaded[q], 16)

            def load_xz(b, th, j):
                e.dma_start(xz[:], x[bass.ds(b, 1), j * P:(j + 1) * P, th * T:(th + 1) * T]
                            .rearrange("o e t -> (o e) t")).then_inc(xz_loaded, 16)

            load_ctx(0, 0)
            load_win(0, 0)
            load_win(1, 1)
            with nc.allow_non_contiguous_dma(reason="small weights, once"):
                for dst, src in (
                    (cw[:], conv_w.rearrange("(j p) k -> p j k", p=P)),
                    (cb[:], conv_b.rearrange("(j p) -> p j", p=P)),
                    (xpw[:], x_projT.rearrange("(j p) k -> p j k", p=P)),
                    (Dv[:], D.rearrange("(j p) -> p j", p=P)),
                    (Av[:].rearrange("p (j n) -> p j n", n=N), A_log.rearrange("(j p) n -> p j n", p=P)),
                    (b1c[0:HD], b1.rearrange("e f -> f e")),
                    (b1c[HD:P], b1.rearrange("e f -> f e")),
                    (b2c[0:HD], b2.rearrange("e d -> d e")),
                    (b2c[HD:P], b2.rearrange("e d -> d e")),
                    (swb[:], sw_b.partition_broadcast(P)),
                    (dtw[B3:B3 + 1], b3.rearrange("(o d) -> o d", o=1)),
                    (dtw[0:DR], dt_projT),
                    (dtw[DR:DR + 1], dt_b),
                ):
                    e.dma_start(dst, src).then_inc(const_loaded, 16)

            for G in range(2, AHEAD + 1):
                if G <= J and G >= 1:
                    k = G - 2
                    if k >= 2:
                        e.wait_ge(row_free[k % 2], 1 + k // 2)
                    load_row(k % 2, x[0:1, k * P:(k + 1) * P, :])
                e.wait_ge(xin_done, 1 + G)
                load_win(G, G % J)
                if G == J:
                    e.wait_ge(xin_done, 1 + J + 1)
                    load_ctx(0, 1)
            e.wait_ge(evac[S], 1 + J // 2 + 1)
            e.dma_start(bc_d[0], bcs).then_inc(bc_stored, 16)
            e.wait_ge(bc_stored, 1 + 16)
            for q in range(PAIRS):
                load_bc(0, q)
            load_xz(0, 0, 0)
            for k in range(J - 1, J):
                e.wait_ge(row_free[k % 2], 1 + k // 2)
                load_row(k % 2, x[0:1, k * P:(k + 1) * P, :])

            def slot(b, plan, t):
                st, q = divmod(t, SLOTS)
                g, c = STEPS * b + st, TH * b + st // J
                if late(plan, t, 3):
                    e.wait_ge(x1_done, 1 + g)
                    settle(e)
                    bo, th, j = chunk_block(st + STEPS - 1)
                    e.dma_start(x1_d[bass.ds(b + bo - 1, 1), th * T:(th + 1) * T, j * P:(j + 1) * P]
                                .rearrange("o (k p) e -> p (o k) e", p=P), xt[:]).then_inc(x1_stored, 16)
                if plan.scan:
                    th, j = divmod(st, J)
                    if q == 1:
                        e.wait_ge(xin_done, 1 + g + AHEAD + 1)
                        settle(e)
                        load_win(st + AHEAD + 1, (st + AHEAD + 1) % J)
                    if q == 2 and j == J - 3:
                        e.wait_ge(xin_done, 1 + g + AHEAD + 2)
                        settle(e)
                        load_ctx(wrap(b + 1), th)
                    if q == 3 and j == J - 2:
                        e.wait_ge(evac[S], 1 + count(plan, b, ("x_proj", th)) + 1)
                        settle(e)
                        e.dma_start(bc_d[bass.ds(c + 1, 1)].rearrange("o n t -> (o n) t"), bcs) \
                            .then_inc(bc_stored, 16)
                    if j == J - 1:
                        if q == 0:
                            e.wait_ge(bc_stored, 1 + 16 * (c + 2))
                            settle(e)
                        e.wait_ge(duB_done, 1 + N * g + 2 * q + 2)
                        settle(e)
                        e.wait_ge(prod_done, 1 + 1 + PAIRS * g + q + 1)
                        settle(e)
                        load_bc(c + 1, q)
                    if q == 5:
                        e.wait_ge(x1_stored, 1 + 16 * g)
                        settle(e)
                        e.dma_start(xt[:], x[bass.ds(b, 1), th * T:(th + 1) * T, j * P:(j + 1) * P]
                                    .rearrange("o (k p) e -> p (o k) e", p=P)).then_inc(xt_loaded, 16)
                    if q == 4:
                        e.wait_ge(zT_done, 1 + g + 1)
                        settle(e)
                        bo, th2, j2 = chunk_block(st + 1)
                        load_xz(wrap(b + 1) if bo else b, th2, j2)
                for what, *a in plan.slots[t]:
                    if what == "row_load":
                        p, filled = row_at(plan, b, tuple(a))
                        e.wait_ge(row_free[p], 1 + filled)
                        settle(e)
                        if a[0] == "ln1":
                            settle(e)
                            load_row(p, x[bass.ds(wrap(b + 1), 1), a[1] * P:(a[1] + 1) * P, :])
                        elif a[0] == "logits":
                            k = a[1]
                            e.wait_ge(x1_stored, 1 + 16 * (STEPS * b if k >= TB else STEPS * b + J))
                            settle(e)
                            load_row(p, x1_d[bass.ds(logit_batch(b, k), 1), k * P:(k + 1) * P, :])
                        else:
                            k = TB * a[1] + a[2]
                            settle(e)
                            load_row(p, x1_d[bass.ds(b - 1, 1), k * P:(k + 1) * P, :])
                    elif what == "sw_load":
                        k, i = a
                        if k == 0 and i == 0 and plan.old:
                            e.wait_ge(sel_step, 1 + 9 * b)
                            settle(e)
                        e.wait_ge(sw_used, 1 + (DI // SD) * f_index(logit_batch(b, k), k) + i)
                        settle(e)
                        e.dma_start(sww[:, i % 2], sw[:, k * P:(k + 1) * P, i * SD:(i + 1) * SD]
                                    .rearrange("e p d -> p e d")).then_inc(sww_loaded[i % 2], 16)
                    elif what == "logit_sum":
                        e.wait_ge(o_done, 1 + 2 * J * (b - 1))
                        settle(e)
                        for i, w in ((0, w1T), (1, w2T)):
                            for lo in (0, HD):
                                e.dma_start(w12[lo:lo + HD, i], w.rearrange("e r c -> r e c")) \
                                    .then_inc(experts_loaded, 16)
                    elif what == "w3_load":
                        n = 2 * NQ * (b - 1) + NQ * a[0] + a[1]
                        e.wait_ge(w3_done, 1 + TB * n)
                        settle(e)
                        e.dma_start(w3q[:], w3T[:, a[1] * QD:(a[1] + 1) * QD].rearrange("(k p) e -> p k e", p=P)) \
                            .then_inc(w3_loaded, 16)
                    elif what == "res_load":
                        uu, i = a
                        qq, k = divmod(i, TB)
                        n = 2 * NQ * (b - 1) + NQ * uu + qq
                        e.wait_ge(out_stored[k], 1 + 16 * n)
                        settle(e)
                        e.dma_start(res[:, k, :], x1_d[bass.ds(b - 1, 1), uu * T + k * P:uu * T + (k + 1) * P,
                                                       qq * QD:(qq + 1) * QD].rearrange("o p d -> p (o d)")) \
                            .then_inc(res_loaded[k], 16)
                    elif what == "tile_out":
                        uu, i = a
                        qq, k = divmod(i, TB)
                        e.wait_ge(evac[bank_of(plan, ("tile", uu, i))], 1 + count(plan, b, ("tile", uu, i)) + 1)
                        settle(e)
                        e.dma_start(out[bass.ds(b - 1, 1), uu * T + k * P:uu * T + (k + 1) * P,
                                        qq * QD:(qq + 1) * QD].rearrange("o p d -> p (o d)"), res[:, k, :]) \
                            .then_inc(out_stored[k], 16)
            turns(e, slot)
            for k in range(TB):
                e.wait_ge(out_stored[k], 1 + 16 * 2 * NQ * NB)

        @block.gpsimd
        def _(pool):
            e = pool
            e.memset(ident[:], 0.0).then_inc(ident_step, 1)
            e.wait_ge(ident_step, 2)
            e.affine_select(out=ident[:], in_=ident[:], compare_op=ALU.not_equal, fill=1.0, base=0,
                            pattern=[[-1, P]], channel_multiplier=1).then_inc(ident_step, 1)
            e.wait_ge(masks, 1 + MASKS)

            def ln1_rstd(b):
                e.wait_ge(ln1_step, 1 + 3 * J * (b + 1))
                e.wait_ge(zn_done, 1 + STEPS * b)
                e.tensor_tensor(r1[:], mv1[:, :, 1], half[:, 0:1].broadcast_to([P, J]), ALU.pow).then_inc(ln1_rs, 1)

            ln1_rstd(0)

            def slot(b, plan, t):
                st, q = divmod(t, SLOTS)
                g, c = STEPS * b + st, TH * b + st // J
                if plan.scan:
                    th, j = divmod(st, J)
                    s = 2 * (q % 2)
                    e.wait_ge(h_done, 1 + RA - 1 + N * g + 2 * q + 2)
                    if th == 0:
                        settle(e)
                        e.tensor_copy(state[:, j * N + 2 * q:j * N + 2 * q + 2], h[:, s:s + 2, T - 1]) \
                            .then_inc(saved, 1)
                    if j == 0:
                        e.wait_ge(bc_loaded[q], 1 + 32 * (c + 1))
                    e.wait_ge(prod_summed, 1 + PAIRS + PAIRS * g + q - 1)
                    e.tensor_tensor(prod[:, s:s + 2, :], h[:, s:s + 2, :], Cb[:, 2 * q:2 * q + 2, :],
                                    ALU.mult).then_inc(prod_done, 1)
                if late(plan, t, 2):
                    e.wait_ge(xt_loaded, 1 + 16 * g)
                    e.wait_ge(yg_done, 1 + g)
                    e.tensor_tensor(xt[:], szT[:], xt[:], ALU.add).then_inc(x1_done, 1)
                for what, *a in plan.slots[t]:
                    if what == "rstd":
                        k = a[0]
                        f = f_index(logit_batch(b, k), k)
                        e.wait_ge(mv_step, 1 + 4 * f + 4)
                        e.tensor_tensor(r2[:, k:k + 1], mv[:, 1:2], half[:, 0:1], ALU.pow).then_inc(rs_done, 1)
                    elif what == "ln1_rstd":
                        ln1_rstd(b + 1)
            turns(e, slot)

        @block.tensor
        def _(pe):
            e = pe

            def in_proj(loads, par, bank, wait):
                e.wait_ge(win_loaded[par], 1 + 16 * loads)
                e.wait_ge(evac[bank], 1 + wait)
                for k in range(DK):
                    mm = e.matmul(dense[:, bank, :], win[:, par, k, :], ctxs[:, k, :],
                                  start=(k == 0), stop=(k == DK - 1))
                mm.then_inc(xin_done, 1)

            def x_proj(c, th, wait):
                e.wait_ge(u_done, 1 + J * (c + 1))
                e.wait_ge(evac[S], 1 + wait)
                for k in range(J):
                    mm = e.matmul(dense[0:DR + 2 * N, S, :], xpw[:, k, :], u[:, J * th + k, :],
                                  start=(k == 0), stop=(k == J - 1))
                mm.then_inc(xdbl_done, 1)

            def before_softplus(c, th, j, wait):
                e.wait_ge(dtrows_done, 1 + c + 1)
                e.wait_ge(evac[S], 1 + wait)
                e.matmul(dense[:, S, :], dtw[0:DR + 1, j * P:(j + 1) * P], dtaug[:, th, :], start=True, stop=True) \
                    .then_inc(v_done, 1)

            def sum_pair(g, q):
                e.wait_ge(prod_done, 1 + 1 + PAIRS * g + q + 1)
                for i in (0, 1):
                    for k in range(TB):
                        mm = e.matmul(yT[:, k, :], prod[:, 2 * (q % 2) + i, k * P:(k + 1) * P], ident[:],
                                      is_transpose=True, start=False, stop=(q == PAIRS - 1 and i == 1),
                                      skip_group_check=True)
                mm.then_inc(prod_summed, 1)

            e.wait_ge(ctx_loaded, 1 + 16)
            for G in range(J):
                in_proj(G // 2 + 1, G % 2, G % 2, G // 2)
            e.wait_ge(const_loaded, 1 + 16 * CONSTS)
            e.wait_ge(masks, 1 + MASKS)
            e.wait_ge(ident_step, 3)
            x_proj(0, 0, J // 2)
            e.wait_ge(ctx_loaded, 1 + 32)
            for G in range(J, AHEAD):
                in_proj(G // 2 + 1, G % 2, G % 2, G // 2 + (1 - G % 2))
            before_softplus(0, 0, 0, AHEAD // 2 + 1)

            def slot(b, plan, t):
                st, q = divmod(t, SLOTS)
                g, c = STEPS * b + st, TH * b + st // J
                if late(plan, t, 0):
                    sum_pair(g - 1, PAIRS - 1)
                if plan.scan:
                    th, j = divmod(st, J)
                    if q == 1:
                        e.wait_ge(yg_done, 1 + g)
                        e.wait_ge(Dd_done, 1 + g + 1)
                        for k in range(TB):
                            e.matmul(yT[:, k, :], u[:, st, k * P:(k + 1) * P], Dd[:], start=(k == 0), stop=False,
                                     skip_group_check=True)
                    if q >= 1:
                        sum_pair(g, q - 1)
                for what, *a in plan.slots[t]:
                    name = (what, *a)
                    if what == "in_proj":
                        if (st + AHEAD) % J == 0:
                            e.wait_ge(ctx_loaded, 1 + 16 * (TH * b + (st + AHEAD) // J + 1))
                        in_proj(STEPS // 2 * b + (st + AHEAD) // 2 + 1, (st + AHEAD) % 2, S, count(plan, b, name))
                    elif what == "x_proj":
                        x_proj(c + 1, 1 - th, count(plan, b, name))
                    elif what == "zT":
                        e.wait_ge(zn_done, 1 + g + 1)
                        e.wait_ge(evac[S], 1 + count(plan, b, name))
                        for k in range(TB):
                            mm = e.transpose(dense[:, S, k * P:(k + 1) * P], xz[:, k * P:(k + 1) * P], ident[:])
                        mm.then_inc(zT_done, 1)
                    elif what == "v":
                        bo, th2, j2 = chunk_block(st + 1)
                        before_softplus(TH * (b + bo) + th2, th2, j2, count(plan, b, name))
                    elif what == "logit":
                        k, i, bank = a
                        f = f_index(logit_batch(b, k), k)
                        if i == 0:
                            e.wait_ge(norm_done, 1 + f + 1)
                            e.wait_ge(evac[bank], 1 + count(plan, b, ("logit", k)))
                        e.wait_ge(sww_loaded[i % 2], 1 + 16 * (f * (DI // SD // 2) + i // 2 + 1))
                        p = row_at(plan, b, ("logits", k))[0]
                        for n in range(SD // 32):
                            lo = i * SD + 32 * n
                            mm = e.matmul(dense[32 * n:32 * n + 32, bank, 0:32 * E], row[:, p, lo:lo + 32],
                                          sww[:, i % 2, :, 32 * n:32 * n + 32],
                                          start=(i == 0), stop=(i == DI // SD - 1))
                        mm.then_inc(sw_used, 1)
                    elif what == "logit_sum":
                        e.wait_ge(lgr_done, 1 + 2 * TB * b)
                        e.wait_ge(evac[F0], 1 + count(plan, b, name))
                        for k in range(2 * TB):
                            mm = e.matmul(dense[:, F0, 0:E], ones[:], lgr[:, k, :], start=(k == 0),
                                          stop=(k == 2 * TB - 1))
                        mm.then_inc(lg_done, 1)
                    elif what == "turn":
                        uu, k = a
                        f = 2 * TB * (b - 1) + TB * uu + k
                        p = row_at(plan, b, name)[0]
                        e.wait_ge(renorm_done, 1 + f + 1)
                        for i in (0, 1):
                            e.wait_ge(evac[F0 + i], 1 + count(plan, b, (*name, i)))
                            for n in range(J // 2):
                                d = (J // 2) * i + n
                                mm = e.transpose(dense[:, F0 + i, n * P:(n + 1) * P], row[:, p, d * P:(d + 1) * P],
                                                 ident[:])
                            mm.then_inc(tr_done, 1)
                    elif what == "hidden":
                        uu, hp = a
                        if hp == 0:
                            e.wait_ge(sel_step, 1 + 9 * b)
                            for i in (0, 1):
                                last = ("turn", uu, TB - 1, i)
                                e.wait_ge(evac[F0 + i], 1 + count(plan, b, last) + 1)
                        for i in (0, 1):
                            e.wait_ge(evac[F0 + i], 1 + count(plan, b, (*name, i)))
                            e.matmul(dense[:, F0 + i, :], w1s[HD * i:HD * i + HD].rearrange("p k f -> p (k f)"),
                                     xT[HD * i:HD * i + HD, hp, :], start=True, stop=True).then_inc(hid_done, 1)
                    elif what == "expert_out":
                        uu, hp = a
                        for i in (0, 1):
                            e.wait_ge(evac[F0 + i], 1 + count(plan, b, ("hidden", uu, hp, i)) + 1)
                        for i in (0, 1):
                            mm = e.matmul(dense[HD * i:HD * i + HD, F0, :], w2s[:], hs[:, i, :],
                                          start=True, stop=True)
                        mm.then_inc(o_done, 1)
                    elif what == "tile":
                        uu, i = a
                        qq, k = divmod(i, TB)
                        bank = bank_of(plan, name)
                        if i == 0:
                            e.wait_ge(evac[F0], 1 + count(plan, b, ("expert_out", uu, J - 1)) + 1)
                        e.wait_ge(w3_loaded, 1 + 16 * (2 * NQ * (b - 1) + NQ * uu + qq + 1))
                        e.wait_ge(evac[bank], 1 + count(plan, b, name))
                        e.matmul(dense[:, bank, 0:QD], ones[B3:B3 + 1, :], dtw[B3:B3 + 1, qq * QD:(qq + 1) * QD],
                                 start=True, stop=False)
                        for d in range(J):
                            mm = e.matmul(dense[:, bank, 0:QD], xT[:, d, k * P:(k + 1) * P], w3q[:, d, :],
                                          start=False, stop=(d == J - 1))
                        mm.then_inc(w3_done, 1)
            turns(e, slot)

        @block.scalar
        def _(act):
            e = act
            e.wait_ge(const_loaded, 1 + 16 * CONSTS)
            e.activation(Av[:], Av[:], ACT.Exp).then_inc(a_ready, 1)

            def pad(G, bank, ready):
                e.wait_ge(conv_step, 1 + 6 * G)
                e.wait_ge(xin_done, 1 + 1 + G + 1)
                e.copy(xpad[:, DC - 1:CH], dense[:, bank, :]).then_inc(evac[bank], 1)

            def silu_u(G, slot_u):
                e.wait_ge(conv_step, 1 + 6 * G + 5)
                e.activation(u[:, slot_u, :], cacc[:], ACT.Silu).then_inc(u_done, 1)

            def split_rows(c, th):
                e.wait_ge(xdbl_done, 1 + c + 1)
                e.copy(dtaug[0:DR, th, :], dense[0:DR, S, :]).then_inc(dtrows_done, 1)
                e.copy(bcs, dense[DR:DR + 2 * N, S, :]).then_inc(evac[S], 1)

            def softplus_a(g):
                e.wait_ge(v_done, 1 + g + 1)
                e.activation(sp[:], dense[:, S, :], ACT.Abs).then_inc(sp_step, 1)
                e.wait_ge(sp_step, 1 + 3 * g + 1)
                e.activation(sp[:], sp[:], ACT.Exp, scale=-1.0).then_inc(sp_step, 1)

            def softplus_b(g):
                e.wait_ge(sp_step, 1 + 3 * g + 2)
                e.activation(sp[:], sp[:], ACT.Ln, bias=1.0).then_inc(sp_step, 1)

            def exp_ln_table(b, plan, after):
                at = plan.table[after]
                if plan is NEXT:
                    at = at + (len(NEXT.table) * (b - 1) + len(FIRST.table))
                e.wait_ge(table_step, 1 + at)
                e.activation(half[:, 2:3], half[:, 1:2], ACT.Ln).then_inc(table_step, 1)

            for G in range(J):
                pad(G, G % 2, None)
                silu_u(G, G)
            split_rows(0, 0)
            for G in range(J, AHEAD):
                pad(G, G % 2, None)
                silu_u(G, G)
            e.wait_ge(masks, 1 + MASKS)
            e.wait_ge(bc_stored, 1 + 16)
            softplus_a(0)
            softplus_b(0)
            e.wait_ge(a_ready, 3)

            def slot(b, plan, t):
                st, q = divmod(t, SLOTS)
                g, c = STEPS * b + st, TH * b + st // J
                if plan.scan:
                    th, j = divmod(st, J)
                    if q == 0:
                        e.wait_ge(prod_summed, 1 + PAIRS * g + 1)
                        e.activation(Dd[:], ident[:], ACT.Copy, scale=Dv[:, j:j + 1]).then_inc(Dd_done, 1)
                        if plan is FIRST and st == 0:
                            e.wait_ge(evac[S], 1 + LEAD_USES[S])
                        elif st == 0:
                            e.wait_ge(evac[S], 1 + NEXT.uses[S] * (b - 1) + LEAD_USES[S] + FIRST.uses[S])
                        else:
                            e.wait_ge(evac[S], 1 + count(plan, b, ("v", st - 1)) + 1)
                    for n in (2 * q, 2 * q + 1):
                        e.wait_ge(h_done, 1 + N * g + n)
                        e.activation(dA[:, n % RA, :], delta[:, st % 2, :], ACT.Exp,
                                     scale=Av[:, j * N + n:j * N + n + 1]).then_inc(dA_done, 1)
                    if q == 1:
                        pad(g + AHEAD, S, None)
                        if st == 0:
                            e.wait_ge(ln1_done, 1 + b + 1)
                        e.wait_ge(xz_loaded, 1 + 16 * (g + 1))
                        e.activation(xz[:], xz[:], ACT.Identity, scale=r1[:, j:j + 1], bias=nm1[:, j:j + 1]) \
                            .then_inc(zn_done, 1)
                    if q == 2 and j == J - 2:
                        split_rows(c + 1, 1 - th)
                    if q == 4:
                        e.wait_ge(du_done, 1 + g)
                        silu_u(g + AHEAD, (st + AHEAD) % UR)
                        e.wait_ge(zT_done, 1 + g + 1)
                        e.wait_ge(x1_done, 1 + g)
                        e.activation(szT[:].rearrange("p k e -> p (k e)"), dense[:, S, :], ACT.Silu) \
                            .then_inc(evac[S], 1)
                        exp_ln_table(b, plan, ("silu", t))
                    if q == 5:
                        if j == J - 2:
                            e.wait_ge(bc_stored, 1 + 16 * (c + 2))
                        softplus_a(g + 1)
                    if q == 6:
                        softplus_b(g + 1)
                for what, *a in plan.slots[t]:
                    name = (what, *a)
                    if what == "norm":
                        k = a[0]
                        f = f_index(logit_batch(b, k), k)
                        p = row_at(plan, b, ("logits", k))[0]
                        e.wait_ge(nm_done, 1 + f + 1)
                        e.activation(row[:, p, :], row[:, p, :], ACT.Identity, scale=r2[:, k:k + 1],
                                     bias=nm2[:, k:k + 1]).then_inc(norm_done, 1)
                    elif what == "route":
                        e.wait_ge(route_step, 1 + 5 * (b - 1) + 2)
                        e.activation(rt[:, 1, :], rt[:, 0, :], ACT.Exp, bias=rt[:, 6, 0:1],
                                     accum_out=rt[:, 6, 1:2]).then_inc(pexp_done, 1)
                    elif what == "renorm":
                        uu, k = a
                        f = 2 * TB * (b - 1) + TB * uu + k
                        p, filled = row_at(plan, b, ("turn", uu, k))
                        e.wait_ge(row_loaded[p], 1 + 16 * (filled + 1))
                        e.activation(row[:, p, :], row[:, p, :], ACT.Identity, scale=r2[:, TB * uu + k:TB * uu + k + 1],
                                     bias=nm2[:, TB * uu + k:TB * uu + k + 1]).then_inc(renorm_done, 1)
                    elif what == "turn":
                        uu, k = a
                        f = 2 * TB * (b - 1) + TB * uu + k
                        for i in (0, 1):
                            e.wait_ge(tr_done, 1 + 2 * f + i + 1)
                            e.wait_ge(w3_done, 1 + 2 * NT * (b - 1) + (NT * uu if uu == 0 else NT * uu - TB + k + 1))
                            e.copy(xT[:, (J // 2) * i:(J // 2) * (i + 1), k * P:(k + 1) * P],
                                   dense[:, F0 + i, :].rearrange("p (d t) -> p d t", t=P)).then_inc(evac[F0 + i], 1)
                    elif what == "hidden":
                        uu, hp = a
                        n = 2 * J * (b - 1) + J * uu + hp
                        e.wait_ge(o_done, 1 + n)
                        if hp == 0:
                            e.wait_ge(sel_step, 1 + 9 * b)
                        for i in (0, 1):
                            e.wait_ge(hid_done, 1 + 2 * n + i + 1)
                            e.activation(hs[:, i, :], dense[:, F0 + i, :], ACT.Gelu, bias=b1s[:]) \
                                .then_inc(evac[F0 + i], 1)
                        if plan.scan:
                            exp_ln_table(b, plan, ("gelu", t))
            turns(e, slot)

        @block.vector
        def _(dve):
            e = dve
            e.memset(ones[:], 1.0).then_inc(masks, 1)
            e.memset(half[:, 0:1], -0.5).then_inc(masks, 1)
            e.memset(half[:, 1:2], 1.0).then_inc(masks, 1)
            e.memset(dtaug[DR:DR + 1], 1.0).then_inc(masks, 1)
            for i in range(E):
                e.memset(iota[:, i:i + 1], float(i)).then_inc(set_up, 1)
            e.wait_ge(ident_step, 3)
            e.wait_ge(set_up, 1 + E)
            e.tensor_copy(diag[:], ident[:, 0:32]).then_inc(set_up, 1)
            for i in range(1, 4):
                e.wait_ge(set_up, 1 + E + i)
                e.tensor_tensor(diag[:], diag[:], ident[:, 32 * i:32 * i + 32], ALU.add).then_inc(set_up, 1)
            e.wait_ge(a_ready, 2)
            e.tensor_scalar(Av[:], Av[:], -1.0, None, ALU.mult).then_inc(a_ready, 1)

            def conv_a(G, bank, evacs, th, j):
                if th == 0:
                    e.memset(xpad[:, 0:DC - 1], 0.0).then_inc(conv_step, 1)
                else:
                    e.tensor_copy(xpad[:, 0:DC - 1], halo[:, j, :]).then_inc(conv_step, 1)
                e.wait_ge(evac[bank], 1 + evacs)
                e.wait_ge(u_done, 1 + G)
                e.tensor_scalar(cacc[:], xpad[:, DC - 1:CH], cw[:, j, DC - 1:DC], cb[:, j:j + 1],
                                ALU.mult, ALU.add).then_inc(conv_step, 1)
                tap(G, 2, j)

            def tap(G, k, j):
                e.wait_ge(conv_step, 1 + 6 * G + DC - k)
                e.scalar_tensor_tensor(out=cacc[:], in0=xpad[:, k:k + T], scalar=cw[:, j, k:k + 1], in1=cacc[:],
                                       op0=ALU.mult, op1=ALU.add).then_inc(conv_step, 1)

            def conv_b(G, j):
                tap(G, 1, j)
                tap(G, 0, j)
                e.tensor_copy(halo[:, j, :], xpad[:, T:CH]).then_inc(conv_step, 1)
                e.wait_ge(conv_step, 1 + 6 * G + 6)

            def ln1_stats(b, k, p, filled):
                n = 3 * J * b + 3 * k
                e.wait_ge(row_loaded[p], 1 + 16 * (filled + 1))
                e.bn_stats(bst[:, 0, :], row[:, p, 0:T]).then_inc(ln1_step, 1)
                e.bn_stats(bst[:, 1, :], row[:, p, T:DI]).then_inc(row_free[p], 1)
                e.wait_ge(ln1_step, 1 + n + 1)
                e.wait_ge(row_free[p], 1 + filled + 1)
                settle(e)
                e.bn_aggr(mv1[:, k, :], bst[:].rearrange("p a b -> p (a b)")).then_inc(ln1_step, 1)
                e.wait_ge(ln1_step, 1 + n + 2)
                e.tensor_scalar(mv1[:, k, 1:2], mv1[:, k, 1:2], EPS, None, ALU.add).then_inc(ln1_step, 1)
                e.wait_ge(ln1_step, 1 + n + 3)

            def ln1_shift(b):
                e.wait_ge(ln1_rs, 1 + b + 1)
                e.scalar_tensor_tensor(out=nm1[:], in0=mv1[:, :, 0], scalar=-1.0, in1=r1[:], op0=ALU.mult,
                                       op1=ALU.mult).then_inc(ln1_done, 1)
                e.wait_ge(ln1_done, 1 + b + 1)

            def softplus_c(g, p, waits):
                e.wait_ge(sp_step, 1 + 3 * g + 3)
                e.scalar_tensor_tensor(out=delta[:, p, :], in0=dense[:, S, :], scalar=0.0, in1=sp[:],
                                       op0=ALU.max, op1=ALU.add).then_inc(evac[S], 1)
                e.wait_ge(evac[S], 1 + waits + 1)

            for G in range(AHEAD):
                evacs = G // 2 + 1 + (1 if G >= J and G % 2 == 0 else 0)
                conv_a(G, G % 2, evacs, G // J, G % J)
                conv_b(G, G % J)
                if G >= 2:
                    ln1_stats(0, G - 2, G % 2, (G - 2) // 2)
            ln1_shift(0)
            softplus_c(0, 0, AHEAD // 2 + 1)

            def slot(b, plan, t):
                st, q = divmod(t, SLOTS)
                g, c = STEPS * b + st, TH * b + st // J
                th, j = divmod(st, J)
                if late(plan, t, 1):
                    e.wait_ge(prod_summed, 1 + PAIRS + PAIRS * g)
                    e.tensor_tensor(szT[:], yT[:], szT[:], ALU.mult).then_inc(yg_done, 1)
                for what, *a in plan.slots[t]:
                    name = (what, *a)
                    if what == "stats":
                        k = a[0]
                        f = f_index(logit_batch(b, k), k)
                        p, filled = row_at(plan, b, ("logits", k))
                        e.wait_ge(row_loaded[p], 1 + 16 * (filled + 1))
                        for i in (0, 1):
                            e.bn_stats(bst[:, i, :], row[:, p, i * T:(i + 1) * T]).then_inc(mv_step, 1)
                        e.wait_ge(mv_step, 1 + 4 * f + 2)
                        settle(e)
                        e.bn_aggr(mv[:], bst[:].rearrange("p a b -> p (a b)")).then_inc(mv_step, 1)
                        e.wait_ge(mv_step, 1 + 4 * f + 3)
                        e.tensor_scalar(mv[:, 1:2], mv[:, 1:2], EPS, None, ALU.add).then_inc(mv_step, 1)
                    elif what == "shift":
                        k = a[0]
                        f = f_index(logit_batch(b, k), k)
                        e.wait_ge(rs_done, 1 + f + 1)
                        e.scalar_tensor_tensor(out=nm2[:, k:k + 1], in0=mv[:, 0:1], scalar=-1.0,
                                               in1=r2[:, k:k + 1], op0=ALU.mult, op1=ALU.mult).then_inc(nm_done, 1)
                        e.wait_ge(nm_done, 1 + f + 1)
                    elif what == "diagonal":
                        k = a[0]
                        f = f_index(logit_batch(b, k), k)
                        bank = bank_of(plan, ("logit", k))
                        e.wait_ge(sw_used, 1 + 1 + (DI // SD) * (f + 1))
                        p, filled = row_at(plan, b, ("logits", k))
                        e.sem_inc(row_free[p], 1)
                        e.tensor_tensor(lgm[:], dense[:, bank, 0:32 * E].rearrange("p (e i) -> p e i", i=32),
                                        diag[:].unsqueeze(1).broadcast_to([P, E, 32]), ALU.mult) \
                            .then_inc(evac[bank], 1)
                        e.wait_ge(evac[bank], 1 + count(plan, b, ("logit", k)) + 1)
                        e.tensor_reduce(lgr[:, k, :], lgm[:], AX.X, ALU.add).then_inc(lgr_done, 1)
                        e.wait_ge(lgr_done, 1 + f + 1)
                    elif what == "turn":
                        f = 2 * TB * (b - 1) + TB * a[0] + a[1]
                        e.wait_ge(tr_done, 1 + 2 * f + 2)
                        e.sem_inc(row_free[row_at(plan, b, name)[0]], 1)
                    elif what == "route":
                        route(b, count(plan, b, ("logit_sum",)))
                    elif what == "expert_out":
                        uu, hp = a
                        e.wait_ge(o_done, 1 + 2 * J * (b - 1) + J * uu + hp + 1)
                        e.scalar_tensor_tensor(out=xT[:, hp, :], in0=dense[:, F0, :], scalar=b2s[:], in1=xT[:, hp, :],
                                               op0=ALU.add, op1=ALU.add).then_inc(evac[F0], 1)
                    elif what == "tile_out":
                        uu, i = a
                        k = i % TB
                        bank = bank_of(plan, ("tile", uu, i))
                        m = 2 * NT * (b - 1) + NT * uu + i
                        e.wait_ge(w3_done, 1 + m + 1)
                        e.wait_ge(res_loaded[k], 1 + 16 * (2 * NQ * (b - 1) + NQ * uu + i // TB + 1))
                        e.tensor_tensor(res[:, k, :], dense[:, bank, 0:QD], res[:, k, :], ALU.add) \
                            .then_inc(evac[bank], 1)
                    elif what == "ln1_stats":
                        ln1_stats(b + 1, a[0], *row_at(plan, b, ("ln1", a[0])))
                    elif what == "ln1_shift":
                        ln1_shift(b + 1)
                if not plan.scan:
                    return
                if q == 2:
                    conv_a(g + AHEAD, S, count(plan, b, ("in_proj", st)) + 1, (st + AHEAD) // J % TH, (st + AHEAD) % J)
                if q == 3:
                    conv_b(g + AHEAD, (st + AHEAD) % J)

                def times_b(n):
                    if n >= 3:
                        e.wait_ge(h_done, 1 + RA - 1 + N * g + n - 2)
                    if j == 0 and n % 2 == 0:
                        e.wait_ge(bc_loaded[n // 2], 1 + 32 * (c + 1))
                    e.tensor_tensor(duB[:, n % 3, :], du[:], Bb[:, n, :], ALU.mult).then_inc(duB_done, 1)

                if q == 0:
                    e.tensor_tensor(du[:], delta[:, st % 2, :], u[:, st, :], ALU.mult).then_inc(du_done, 1)
                    e.wait_ge(du_done, 1 + g + 1)
                    times_b(0)
                for n in (2 * q, 2 * q + 1):
                    if n + 1 < N:
                        times_b(n + 1)
                    e.wait_ge(duB_done, 1 + N * g + n + 1)
                    e.wait_ge(dA_done, 1 + N * g + n + 1)
                    if n % 2 == 0:
                        e.wait_ge(prod_done, 1 + 1 + PAIRS * g + q - 1)
                    if th:
                        e.wait_ge(saved, 1 + PAIRS * (J * (b + 1)))
                    e.tensor_tensor_scan(h[:, n % 4, :], dA[:, n % RA, :], duB[:, n % 3, :],
                                         state[:, j * N + n:j * N + n + 1] if th else 0.0, ALU.mult, ALU.add) \
                        .then_inc(h_done, 1)
                if q == SLOTS - 1:
                    e.wait_ge(h_done, 1 + RA - 1 + N * (g + 1))
                    softplus_c(g + 1, (st + 1) % 2, count(plan, b, ("v", st)))

            def route(b, before):
                r, n = 5 * (b - 1), 9 * (b - 1)
                e.wait_ge(lg_done, 1 + b)
                e.tensor_tensor(rt[:, 0, :], dense[:, F0, 0:E], swb[:], ALU.add).then_inc(evac[F0], 1)
                e.wait_ge(evac[F0], 1 + before + 1)
                settle(e)
                e.max(rt[:, 4, :], rt[:, 0, :]).then_inc(route_step, 1)
                e.wait_ge(route_step, 1 + r + 1)
                e.tensor_scalar(rt[:, 6, 0:1], rt[:, 4, 0:1], -1.0, None, ALU.mult).then_inc(route_step, 1)
                e.wait_ge(pexp_done, 1 + b)
                e.reciprocal(rt[:, 6, 2:3], rt[:, 6, 1:2]).then_inc(route_step, 1)
                e.wait_ge(route_step, 1 + r + 3)
                e.tensor_scalar(rt[:, 2, :], rt[:, 1, :], rt[:, 6, 2:3], None, ALU.mult).then_inc(route_step, 1)
                e.wait_ge(route_step, 1 + r + 4)
                settle(e)
                e.max(rt[:, 3, :], rt[:, 2, :]).then_inc(route_step, 1)
                e.wait_ge(route_step, 1 + r + 5)
                settle(e)
                e.max_index(idx[:], rt[:, 3, :], rt[:, 2, :]).then_inc(top_step, 1)
                e.wait_ge(top_step, 1 + 9 * (b - 1) + 1)
                e.tensor_copy(rt[:, 5, :], idx[:]).then_inc(top_step, 1)
                e.wait_ge(top_step, 1 + 9 * (b - 1) + 2)
                for i in (0, 1):
                    e.tensor_scalar(hot[:, i, :], iota[:], rt[:, 5, i:i + 1], None, ALU.is_equal).then_inc(top_step, 1)
                    lo = HD * i
                    e.tensor_scalar(hot[lo:lo + HD, 2, :], iota[lo:lo + HD], rt[lo:lo + HD, 5, i:i + 1], None,
                                    ALU.is_equal).then_inc(top_step, 1)
                    e.tensor_scalar(hot[lo:lo + HD, 3, :], iota[lo:lo + HD], rt[lo:lo + HD, 5, i:i + 1],
                                    rt[lo:lo + HD, 3, i:i + 1], ALU.is_equal, ALU.mult).then_inc(top_step, 1)
                e.wait_ge(top_step, 1 + 9 * (b - 1) + 8)
                e.tensor_scalar(rt[:, 4, :], hot[:, 0, :], rt[:, 3, 0:1], None, ALU.mult).then_inc(top_step, 1)
                e.wait_ge(top_step, 1 + 9 * (b - 1) + 9)
                e.scalar_tensor_tensor(out=rt[:, 4, :], in0=hot[:, 1, :], scalar=rt[:, 3, 1:2], in1=rt[:, 4, :],
                                       op0=ALU.mult, op1=ALU.add).then_inc(sel_step, 1)
                e.wait_ge(experts_loaded, 1 + 64 * b)
                done = 1
                for src, on, dst in ((w12[:, 0], hot[:, 0, :], w1s[:, 0, :]), (w12[:, 0], hot[:, 1, :], w1s[:, 1, :]),
                                     (w12[:, 1], hot[:, 3, :], w2s[:])):
                    e.wait_ge(sel_step, 1 + n + done)
                    e.tensor_tensor(wt, src, on.unsqueeze(2).broadcast_to([P, E, HD]), ALU.mult) \
                        .then_inc(sel_step, 1)
                    e.wait_ge(sel_step, 1 + n + done + 1)
                    e.tensor_reduce(dst, wt.rearrange("p e f -> p f e"), AX.X, ALU.add).then_inc(sel_step, 1)
                    done += 2
                e.tensor_tensor_reduce(lgm[:, :, 0], b1c[:], hot[:, 2, :], 1.0, 0.0, ALU.mult, ALU.add,
                                       b1s[:]).then_inc(sel_step, 1)
                e.wait_ge(sel_step, 1 + n + 8)
                e.tensor_tensor_reduce(lgm[:, :, 0], b2c[:], rt[:, 4, :], 1.0, 0.0, ALU.mult, ALU.add,
                                       b2s[:]).then_inc(sel_step, 1)
                e.wait_ge(sel_step, 1 + n + 9)

            turns(e, slot)


def kernel(**inputs):
    import numpy as _np
    import concourse.bacc as _bacc
    from concourse import mybir as _mybir
    from concourse.bass_utils import run_bass_kernel_spmd as _run

    def get(name):
        return _np.asarray(inputs[name])

    laid = {
        "x": get("x"),
        "ctxT": get("ctx_1024").transpose(0, 2, 1),
        "w_inT": get("L0_xattn_in_proj_w").T,
        "conv_w": get("L0_xattn_conv_w"),
        "conv_b": get("L0_xattn_conv_b"),
        "x_projT": get("L0_xattn_x_proj_w").T,
        "dt_projT": get("L0_xattn_dt_proj_w").T,
        "dt_b": get("L0_xattn_dt_proj_b").reshape(1, -1),
        "A_log": get("L0_xattn_A_log"),
        "D": get("L0_xattn_D"),
        "sw": get("L0_ffn_switch_w").reshape(E, L, DI),
        "sw_b": get("L0_ffn_switch_b"),
        "w1T": get("L0_ffn_w1").transpose(0, 2, 1),
        "b1": get("L0_ffn_b1"),
        "w2T": get("L0_ffn_w2").transpose(0, 2, 1),
        "b2": get("L0_ffn_b2"),
        "w3T": get("L0_ffn_w3").T,
        "b3": get("L0_ffn_b3"),
    }
    nc = _bacc.Bacc("TRN2", target_bir_lowering=False, num_devices=1)
    arrays, args = {}, []
    for name, a in laid.items():
        a = _np.ascontiguousarray(a)
        arrays[f"in_{name}"] = a
        args.append(nc.dram_tensor(f"in_{name}", a.shape, _mybir.dt.from_np(a.dtype), kind="ExternalInput").ap())
    args.append(nc.dram_tensor("out_0", (NB, L, DI), _mybir.dt.float32, kind="ExternalOutput").ap())
    build(nc, *args)
    r = _run(nc, [arrays], core_ids=[0])
    return r.results[0]["out_0"]
```

```python
from contextlib import ExitStack

import concourse.bass as bass
from concourse import mybir

F32 = mybir.dt.float32
U32 = mybir.dt.uint32
ALU = mybir.AluOpType
ACT = mybir.ActivationFunctionType
AX = mybir.AxisListType

P = 128
NB, L, DI, DM = 4, 1024, 1024, 512
T = 512
TH = L // T
TB = T // P
J = DI // P
N = 16
DR = 32
DC = 4
E = 8
HD = 64
DK = DM // P
EPS = 1e-5
PAIRS = N // 2
CH = T + DC - 1
SD = 128
SWL = DI // SD
SW0 = 4
QD = 128
NQ = DI // QD
B3 = 64
RA = 4
RH = 3
SLOTS = PAIRS
STEPS = TH * J
AHEAD = 10
UR = 2 * J
S, F0, F1, F2 = 0, 1, 2, 3


class Plan:

    def __init__(self, scan, old):
        self.scan, self.old = scan, old
        self.slots = [[] for _ in range(STEPS * SLOTS)]
        rows = []
        if scan:
            for st in range(STEPS):
                t = SLOTS * st
                self.add(t + 1, "v", st)
                if st % J == J - 2:
                    self.add(t + 3, "x_proj", st // J)
                    self.add(t + 4, "x_proj_end", st // J)
                self.add(t + 4, "in_proj", st)
                self.add(t + 6, "zT", st)
            for k in range(J):
                rows.append((42 + 4 * k, "ln1", k))
                self.add(45 + 4 * k, "ln1_stats", k)
            self.add(124, "ln1_rstd")
            self.add(126, "ln1_shift")
        if old:
            for k in range(TB):
                self.logits(TB + k, [4, 5, 17, 22][k], 9 + 5 * k, 3, rows, F0 + k % 2)
            self.add(33, "logit_sum")
            self.add(34, "route")
            for u, turned, hidden, tiles in (
                (0, [35, 37, 40, 42], 44, 63),
                (1, [81, 83, 86, 88], 90, 107),
            ):
                for k in range(TB):
                    rows.append((turned[k] - 4, "turn", u, k))
                    self.add(turned[k] - 1, "renorm", u, k)
                    self.add(turned[k], "turn", u, k)
                    self.add(turned[k] + 2, "turned", u, k)
                for hp in range(J):
                    self.add(hidden + 2 * hp + 2, "expert_out", u, hp)
                    self.add(hidden + 2 * hp + 4, "out_add", u, hp)
                for hp in range(J):
                    self.add(hidden + 2 * hp, "hidden", u, hp)
                    self.add(hidden + 2 * hp + 2, "gelu", u, hp)
                for i in range(NQ):
                    at = [tiles + 9 * (TB * i + k) // 16 for k in range(TB)]
                    self.add(at[0] - 2, "w3_load", u, i)
                    self.add(at[0], "res_load", u, i)
                    for k in range(TB):
                        self.add(at[k], "tile", u, i, k)
                    self.add(at[-1] + 3, "tile_out", u, i)
        if scan:
            for k in range(TB):
                self.logits(k, 100 + 5 * k, 104 + 5 * k - (k == 3), 3, rows, F2)
        self.row = {}
        for i, (t, *what) in enumerate(sorted(rows, key=lambda r: r[0])):
            self.row[tuple(what)] = i
            self.slots[t].insert(0, ("row_load", *what))
        self.rows = len(rows)
        self.use, self.uses = {}, [0, 0, 0, 0]
        for slot in self.slots:
            for what, *args in slot:
                for name, bank in self.banks(what, args):
                    self.use[name] = (bank, self.uses[bank])
                    self.uses[bank] += 1

    def add(self, t, *what):
        self.slots[t].append(what)

    def logits(self, k, load, t, span, rows, bank):
        rows.append((load, "logits", k))
        self.add(t, "stats", k)
        self.add(t, "rstd", k)
        self.add(t + 2, "shift", k)
        self.add(t + 3, "norm", k)
        loads = SWL
        for i in range(loads):
            at = t + 3 + i * span // loads
            self.add(at - 1, "sw_load", k, i)
            self.add(at, "logit", k, i, bank)
        self.add(t + 5 + span, "diagonal", k)

    @staticmethod
    def banks(what, args):
        if what in ("in_proj", "x_proj", "zT", "v"):
            return [((what, *args), S)]
        if what == "logit" and args[1] == 0:
            return [(("logit", args[0]), args[2])]
        if what == "logit_sum":
            return [(("logit_sum",), F2)]
        if what in ("turn", "hidden"):
            return [((what, *args, 0), F0), ((what, *args, 1), F1)]
        if what == "expert_out":
            return [((what, *args), F2)]
        if what == "tile" and args[2] == 0:
            return [(("tile", *args[:2]), F0 + args[1] % 2)]
        return []


FIRST, NEXT, LAST = Plan(True, False), Plan(True, True), Plan(False, True)
LEAD_USES = (AHEAD // 2 + 2, AHEAD // 2, 0, 0)


def build(nc, x, ctxT, w_inT, conv_w, conv_b, x_projT, dt_projT, dt_b, A_log, D, sw, sw_b,
          w1T, b1, w2T, b2, w3T, b3, out):
    x1_d = nc.dram_tensor("x1_scratch", (NB, L, DI), F32, kind="Internal").ap()
    bc_d = nc.dram_tensor("bc_scratch", (NB * TH + 1, 2 * N, T), F32, kind="Internal").ap()

    with ExitStack() as ctx:
        def sb(name, shape, dt=F32):
            return ctx.enter_context(nc.sbuf_tensor(name, shape, dt))

        counts = []

        def sem(name, start=0):
            s = ctx.enter_context(nc.semaphore(name))
            counts.append((s, 1 + start))
            return s

        ident = sb("ident", [P, P])
        ones = sb("ones", [P, P])
        diag = sb("diag", [P, 32])
        iota = sb("iota", [P, E])
        half = sb("half", [P, 1])
        xpw = sb("xpw", [P, J, DR + 2 * N])
        dtw = sb("dtw", [B3 + 1, DI])
        cw = sb("cw", [P, J, DC])
        cb = sb("cb", [P, J])
        Dv = sb("Dv", [P, J])
        Av = sb("Av", [P, J * N])
        b1c = sb("b1c", [P, E])
        b2c = sb("b2c", [P, E])
        swb = sb("swb", [P, E])
        ctxs = sb("ctxs", [P, DK, T])
        win = sb("win", [P, 2, DK, P])
        xpad = sb("xpad", [P, CH])
        halo = sb("halo", [P, J, DC - 1])
        cacc = sb("cacc", [P, T])
        u = sb("u", [P, UR, T])
        dtaug = sb("dtaug", [DR + 1, TH, T])
        Bb = sb("Bb", [P, N, T])
        Cb = sb("Cb", [P, N, T])
        du = sb("du", [P, T])
        delta = sb("delta", [P, 2, T])
        dA = sb("dA", [P, RA, T])
        h = sb("h", [P, 2 * RH, T])
        state = sb("state", [P, J * N])
        Dd = sb("Dd", [P, P])
        xz = sb("xz", [P, T])
        szT = sb("szT", [P, TB, P])
        xt = sb("xt", [P, TB, P])
        mv1 = sb("mv1", [P, J, 2])
        r1 = sb("r1", [P, J])
        nm1 = sb("nm1", [P, J])
        row = sb("row", [P, 2, DI])
        bst = sb("bst", [P, 2, 6])
        mv = sb("mv", [P, 2])
        r2 = sb("r2", [P, 2 * TB])
        nm2 = sb("nm2", [P, 2 * TB])
        sww = sb("sww", [P, 2, E, SD])
        lgm = sb("lgm", [P, E, 32])
        lgr = sb("lgr", [P, 2 * TB, E])
        rt = sb("rt", [P, 7, E])
        idx = sb("idx", [P, E], U32)
        hot = sb("hot", [P, 4, E])
        w1s = sb("w1s", [P, 2, HD])
        w2s = sb("w2s", [P, HD])
        b1s = sb("b1s", [P, 1])
        b2s = sb("b2s", [P, 1])
        xT = sb("xT", [P, J, T])
        hs = sb("hs", [P, 2, T])
        w3q = sb("w3q", [P, 2, J, QD])
        res = sb("res", [P, 2, TB, QD])
        bcs = cacc[DR:DR + 2 * N, :]
        w12 = hs[:].rearrange("p i (e f) -> p i e f", e=E)
        sw_ring = [sww[:, 0], sww[:, 1], hs[:].rearrange("p i (e d) -> p (i e) d", d=SD),
                w3q[:, 0], w3q[:, 1]]
        wt = sww[:, 0].rearrange("p e s -> p (e s)")[:, 0:E * HD].rearrange("p (e f) -> p e f", e=E)

        duB = ctx.enter_context(nc.psum_tensor("duB", [P, 3, T], F32))
        yT = ctx.enter_context(nc.psum_tensor("yT", [P, TB, P], F32))
        dense = ctx.enter_context(nc.psum_tensor("dense", [P, 4, T], F32))

        const_loaded = sem("const_loaded")
        ctx_loaded = sem("ctx_loaded")
        win_loaded = [sem(f"win_loaded{p}") for p in (0, 1)]
        bc_stored = sem("bc_stored")
        bc_loaded = [sem(f"bc_loaded{q}") for q in range(PAIRS)]
        xz_loaded = sem("xz_loaded")
        xt_loaded = sem("xt_loaded")
        x1_stored = sem("x1_stored")
        row_loaded = [sem(f"row_loaded{p}") for p in (0, 1)]
        sww_loaded = [sem(f"sww_loaded{p}") for p in range(3)]
        sww_loaded5 = [sem(f"sww_loaded5_{p}") for p in range(5)]
        experts_loaded = sem("experts_loaded")
        w3_loaded = [sem(f"w3_loaded{p}") for p in (0, 1)]
        res_loaded = [sem(f"res_loaded{p}") for p in (0, 1)]
        out_stored = [sem(f"out_stored{p}") for p in (0, 1)]
        set_up = sem("set_up")
        ident_step = sem("ident_step")
        masks = sem("masks")
        a_ready = sem("a_ready")
        evac = [sem(f"evac{s}") for s in range(4)]
        xin_done = sem("xin_done", start=1)
        conv_step = sem("conv_step")
        u_done = sem("u_done")
        xdbl_done = sem("xdbl_done")
        dtrows_done = sem("dtrows_done")
        v_done = sem("v_done")
        sp_step = sem("sp_step")
        du_done = sem("du_done")
        dA_done = sem("dA_done")
        duB_done = sem("duB_done")
        h_done = sem("h_done", start=RA - 1)
        saved = sem("saved")
        prod_done = sem("prod_done", start=1)
        prod_summed = sem("prod_summed", start=PAIRS)
        Dd_done = sem("Dd_done")
        zn_done = sem("zn_done")
        zT_done = sem("zT_done")
        yg_done = sem("yg_done")
        x1_done = sem("x1_done")
        ln1_step = sem("ln1_step")
        ln1_rs = sem("ln1_rs")
        ln1_done = sem("ln1_done")
        row_free = [sem(f"row_free{p}") for p in (0, 1)]
        mv_step = sem("mv_step")
        rs_done = sem("rs_done")
        nm_done = sem("nm_done")
        norm_done = sem("norm_done")
        sw_used = sem("sw_used", start=SW0)
        lgr_done = sem("lgr_done")
        lg_done = sem("lg_done")
        route_step = sem("route_step")
        pexp_done = sem("pexp_done")
        top_step = sem("top_step")
        sel_step = sem("sel_step")
        renorm_done = sem("renorm_done")
        tr_done = sem("tr_done")
        hid_done = sem("hid_done")
        o_done = sem("o_done")
        w3_done = sem("w3_done", start=1)
        settled = sem("settled")

        CONSTS = 13
        MASKS = 3
        for s_, start in counts:
            nc.sync.sem_inc(s_, start)
        nc.all_engine_barrier()
        block = ctx.enter_context(nc.Block())

        def settle(eng):
            eng.sem_inc(settled, 1)

        def turns(eng, slot):
            for t in range(STEPS * SLOTS):
                slot(0, FIRST, t)
            with eng.Fori(1, NB) as b:
                for t in range(STEPS * SLOTS):
                    slot(b, NEXT, t)
            for t in range(STEPS * SLOTS):
                slot(NB, LAST, t)

        def count(plan, b, name):
            bank, at = plan.use[name]
            if plan is FIRST:
                return LEAD_USES[bank] + at
            return NEXT.uses[bank] * (b - 1) + (LEAD_USES[bank] + FIRST.uses[bank] + at)

        def filled_last_step(plan, b, st, what):
            if st:
                return count(plan, b, (what, st - 1)) + 1
            return NEXT.uses[S] * (b - 1) + (LEAD_USES[S] + FIRST.use[(what, STEPS - 1)][1] + 1)

        def bank_of(plan, name):
            return plan.use[name][0]

        def row_at(plan, b, what):
            i = plan.row[what]
            if plan is FIRST:
                return i % 2, J // 2 + i // 2
            return i % 2, NEXT.rows // 2 * (b - 1) + (J // 2 + FIRST.rows // 2 + i // 2)

        def late(plan, t, q):
            return t % SLOTS == q and (t >= SLOTS or plan is not FIRST) and (plan.scan or t < SLOTS)

        def chunk_block(G):
            return G // STEPS, G // J % TH, G % J

        def wrap(b):
            return b % NB

        def f_index(b, k):
            return 2 * TB * b + k

        def sw_bufs(k):
            return 5 if k >= TB else 3

        def sw_sem(k):
            return sww_loaded5 if k >= TB else sww_loaded

        def logit_batch(b, k):
            return b - 1 if k >= TB else b

        @block.sync
        def _(sync):
            e = sync

            def load_row(p, src):
                e.dma_start(row[:, p, :], src.rearrange("o p d -> p (o d)")).then_inc(row_loaded[p], 16)

            def load_win(G, j):
                e.dma_start(win[:, G % 2], w_inT[j]) \
                    .then_inc(win_loaded[G % 2], 16)

            def load_ctx(b, th):
                e.dma_start(ctxs[:], ctxT[bass.ds(b, 1), :, th * T:(th + 1) * T]
                            .rearrange("o (k p) t -> p (o k) t", p=P)).then_inc(ctx_loaded, 16)

            def load_bc(c, q):
                for i, dst in ((0, Bb), (N, Cb)):
                    e.dma_start(dst[:, 2 * q:2 * q + 2, :], bc_d[bass.ds(c, 1), i + 2 * q:i + 2 * q + 2, :]
                                .rearrange("o n t -> (o n) t").partition_broadcast(P)).then_inc(bc_loaded[q], 16)

            def load_xz(b, th, j):
                e.dma_start(xz[:], x[bass.ds(b, 1), j * P:(j + 1) * P, th * T:(th + 1) * T]
                            .rearrange("o e t -> (o e) t")).then_inc(xz_loaded, 16)

            load_ctx(0, 0)
            load_win(0, 0)
            load_win(1, 1)
            with nc.allow_non_contiguous_dma(reason="small weights, once"):
                for dst, src in (
                    (cw[:], conv_w.rearrange("(j p) k -> p j k", p=P)),
                    (cb[:], conv_b.rearrange("(j p) -> p j", p=P)),
                    (xpw[:], x_projT.rearrange("(j p) k -> p j k", p=P)),
                    (Dv[:], D.rearrange("(j p) -> p j", p=P)),
                    (Av[:].rearrange("p (j n) -> p j n", n=N), A_log.rearrange("(j p) n -> p j n", p=P)),
                    (b1c[0:HD], b1.rearrange("e f -> f e")),
                    (b1c[HD:P], b1.rearrange("e f -> f e")),
                    (b2c[0:HD], b2.rearrange("e d -> d e")),
                    (b2c[HD:P], b2.rearrange("e d -> d e")),
                    (swb[:], sw_b.partition_broadcast(P)),
                    (dtw[B3:B3 + 1], b3.rearrange("(o d) -> o d", o=1)),
                    (dtw[0:DR], dt_projT),
                    (dtw[DR:DR + 1], dt_b),
                ):
                    e.dma_start(dst, src).then_inc(const_loaded, 16)

            for G in range(2, AHEAD + 1):
                if G <= J and G >= 1:
                    k = G - 2
                    if k >= 2:
                        e.wait_ge(row_free[k % 2], 1 + k // 2)
                    load_row(k % 2, x[0:1, k * P:(k + 1) * P, :])
                e.wait_ge(xin_done, 1 + G)
                load_win(G, G % J)
                if G == J:
                    e.wait_ge(xin_done, 1 + J + 1)
                    load_ctx(0, 1)
            e.wait_ge(evac[S], 1 + J // 2 + 1)
            e.dma_start(bc_d[0], bcs).then_inc(bc_stored, 16)
            e.wait_ge(bc_stored, 1 + 16)
            for q in range(PAIRS):
                load_bc(0, q)
            load_xz(0, 0, 0)
            for k in range(J - 1, J):
                e.wait_ge(row_free[k % 2], 1 + k // 2)
                load_row(k % 2, x[0:1, k * P:(k + 1) * P, :])

            def reload_bc(g, c, q):
                if q == 0:
                    e.wait_ge(bc_stored, 1 + 16 * (c + 1))
                    settle(e)
                e.wait_ge(duB_done, 1 + N * g + 2 * q + 2)
                settle(e)
                e.wait_ge(prod_done, 1 + 1 + PAIRS * g + q + 1)
                settle(e)
                load_bc(c, q)

            def slot(b, plan, t):
                st, q = divmod(t, SLOTS)
                g, c = STEPS * b + st, TH * b + st // J
                if late(plan, t, 4):
                    e.wait_ge(x1_done, 1 + g)
                    settle(e)
                    bo, th, j = chunk_block(st + STEPS - 1)
                    e.dma_start(x1_d[bass.ds(b + bo - 1, 1), th * T:(th + 1) * T, j * P:(j + 1) * P]
                                .rearrange("o (k p) e -> p (o k) e", p=P), xt[:]).then_inc(x1_stored, 16)
                if plan.scan:
                    th, j = divmod(st, J)
                    if q == 5:
                        e.wait_ge(xin_done, 1 + g + AHEAD + 1)
                        settle(e)
                        load_win(st + AHEAD + 1, (st + AHEAD + 1) % J)
                    if q == 6 and j == J - 3:
                        e.wait_ge(xin_done, 1 + g + AHEAD + 2)
                        settle(e)
                        load_ctx(wrap(b + 1), th)
                    if q == 5 and j == J - 2:
                        e.wait_ge(evac[S], 1 + count(plan, b, ("x_proj", th)) + 1)
                        settle(e)
                        e.dma_start(bc_d[bass.ds(c + 1, 1)].rearrange("o n t -> (o n) t"), bcs) \
                            .then_inc(bc_stored, 16)
                    if j == J - 1 and q >= 2:
                        reload_bc(g, c + 1, q - 2)
                    if j == 0 and q < 2 and late(plan, t, q):
                        reload_bc(g - 1, c, PAIRS - 2 + q)
                    if q == 6:
                        e.wait_ge(x1_stored, 1 + 16 * g)
                        settle(e)
                        e.dma_start(xt[:], x[bass.ds(b, 1), th * T:(th + 1) * T, j * P:(j + 1) * P]
                                    .rearrange("o (k p) e -> p (o k) e", p=P)).then_inc(xt_loaded, 16)
                    if q == 7:
                        e.wait_ge(zT_done, 1 + g + 1)
                        settle(e)
                        bo, th2, j2 = chunk_block(st + 1)
                        load_xz(wrap(b + 1) if bo else b, th2, j2)
                for what, *a in plan.slots[t]:
                    if what == "row_load":
                        p, filled = row_at(plan, b, tuple(a))
                        e.wait_ge(row_free[p], 1 + filled)
                        settle(e)
                        if a[0] == "ln1":
                            load_row(p, x[bass.ds(wrap(b + 1), 1), a[1] * P:(a[1] + 1) * P, :])
                        elif a[0] == "logits":
                            k = a[1]
                            e.wait_ge(x1_stored, 1 + 16 * (STEPS * b if k >= TB else STEPS * b + J))
                            settle(e)
                            load_row(p, x1_d[bass.ds(logit_batch(b, k), 1), k * P:(k + 1) * P, :])
                        else:
                            k = TB * a[1] + a[2]
                            settle(e)
                            load_row(p, x1_d[bass.ds(b - 1, 1), k * P:(k + 1) * P, :])
                    elif what == "sw_load":
                        k, i = a
                        if k == 0 and i == 0 and plan.old:
                            e.wait_ge(sel_step, 1 + 9 * b)
                            settle(e)
                        if k == 0 and i == 2 and plan.old:
                            e.wait_ge(o_done, 1 + 2 * J * b)
                            settle(e)
                        if k == TB and i == 3:
                            e.wait_ge(w3_done, 1 + 1 + 2 * NQ * (b - 1))
                            settle(e)
                        ring = sw_bufs(k)
                        free = i + 1 - ring if i >= ring else i + 1 + (SWL - 1 - i) // ring * ring - SWL
                        if k % TB == 0 and i < ring:
                            free = 0
                        if k % TB or i == 0 or i >= ring:
                            e.wait_ge(sw_used, 1 + SW0 + SWL * f_index(logit_batch(b, k), k) + free)
                            settle(e)
                        e.dma_start(sw_ring[i % ring], sw[k * P:(k + 1) * P, i]).then_inc(sw_sem(k)[i % ring], 16)
                    elif what == "logit_sum":
                        e.wait_ge(sw_used, 1 + SW0 + SWL * 2 * TB * b)
                        settle(e)
                        for i, w in ((0, w1T), (1, w2T)):
                            for lo in (0, HD):
                                e.dma_start(w12[lo:lo + HD, i], w.rearrange("e r c -> r e c")) \
                                    .then_inc(experts_loaded, 16)
                    elif what == "w3_load":
                        uu, i = a
                        n = 2 * NQ * (b - 1) + NQ * uu + i
                        e.wait_ge(w3_done, 1 + n)
                        settle(e)
                        e.dma_start(w3q[:, i % 2], w3T[i]) \
                            .then_inc(w3_loaded[i % 2], 16)
                    elif what == "res_load":
                        uu, i = a
                        e.wait_ge(out_stored[i % 2], 1 + 16 * (NQ * (b - 1) + NQ // 2 * uu + i // 2))
                        settle(e)
                        e.dma_start(res[:, i % 2], x1_d[bass.ds(b - 1, 1), uu * T:(uu + 1) * T, i * QD:(i + 1) * QD]
                                    .rearrange("o (k p) d -> p (o k) d", p=P)).then_inc(res_loaded[i % 2], 16)
                    elif what == "tile_out":
                        uu, i = a
                        e.wait_ge(evac[bank_of(plan, ("tile", uu, i))], 1 + count(plan, b, ("tile", uu, i)) + 1)
                        settle(e)
                        e.dma_start(out[bass.ds(b - 1, 1), uu * T:(uu + 1) * T, i * QD:(i + 1) * QD]
                                    .rearrange("o (k p) d -> p (o k) d", p=P), res[:, i % 2]) \
                            .then_inc(out_stored[i % 2], 16)
            turns(e, slot)
            for p in (0, 1):
                e.wait_ge(out_stored[p], 1 + 16 * NQ * NB)

        @block.gpsimd
        def _(pool):
            e = pool
            e.memset(ident[:], 0.0).then_inc(ident_step, 1)
            e.wait_ge(ident_step, 2)
            e.affine_select(out=ident[:], in_=ident[:], compare_op=ALU.not_equal, fill=1.0, base=0,
                            pattern=[[-1, P]], channel_multiplier=1).then_inc(ident_step, 1)
            e.wait_ge(masks, 1 + MASKS)

            def ln1_rstd(b):
                e.wait_ge(ln1_step, 1 + 3 * J * (b + 1))
                e.wait_ge(zn_done, 1 + STEPS * b)
                e.tensor_tensor(r1[:], mv1[:, :, 1], half[:, 0:1].broadcast_to([P, J]), ALU.pow).then_inc(ln1_rs, 1)

            ln1_rstd(0)

            def slot(b, plan, t):
                st, q = divmod(t, SLOTS)
                g, c = STEPS * b + st, TH * b + st // J
                if late(plan, t, 3):
                    e.wait_ge(xt_loaded, 1 + 16 * g)
                    e.wait_ge(yg_done, 1 + g)
                    e.tensor_tensor(xt[:], szT[:], xt[:], ALU.add).then_inc(x1_done, 1)
                if plan.scan:
                    th, j = divmod(st, J)
                    s = 2 * (q % RH)
                    e.wait_ge(h_done, 1 + RA - 1 + N * g + 2 * q + 2)
                    if th == 0:
                        settle(e)
                        e.tensor_copy(state[:, j * N + 2 * q:j * N + 2 * q + 2], h[:, s:s + 2, T - 1]) \
                            .then_inc(saved, 1)
                    if j == 0:
                        e.wait_ge(bc_loaded[q], 1 + 32 * (c + 1))
                        settle(e)
                    if th == 0:
                        e.wait_ge(saved, 1 + PAIRS * (J * b + j) + q + 1)
                    e.tensor_tensor(h[:, s:s + 2, :], h[:, s:s + 2, :], Cb[:, 2 * q:2 * q + 2, :],
                                    ALU.mult).then_inc(prod_done, 1)
                for what, *a in plan.slots[t]:
                    if what == "rstd":
                        k = a[0]
                        f = f_index(logit_batch(b, k), k)
                        e.wait_ge(mv_step, 1 + 4 * f + 4)
                        e.tensor_tensor(r2[:, k:k + 1], mv[:, 1:2], half[:, 0:1], ALU.pow).then_inc(rs_done, 1)
                    elif what == "ln1_rstd":
                        ln1_rstd(b + 1)
            turns(e, slot)

        @block.tensor
        def _(pe):
            e = pe

            def in_proj(loads, par, bank, wait):
                e.wait_ge(win_loaded[par], 1 + 16 * loads)
                e.wait_ge(evac[bank], 1 + wait)
                for k in range(DK):
                    mm = e.matmul(dense[:, bank, :], win[:, par, k, :], ctxs[:, k, :],
                                  start=(k == 0), stop=(k == DK - 1))
                mm.then_inc(xin_done, 1)

            def x_proj(c, th, wait):
                e.wait_ge(u_done, 1 + J * (c + 1))
                e.wait_ge(evac[S], 1 + wait)
                x_proj_part(th, range(J // 2))

            def x_proj_part(th, blocks):
                for k in blocks:
                    mm = e.matmul(dense[0:DR + 2 * N, S, :], xpw[:, k, :], u[:, J * th + k, :],
                                  start=(k == 0), stop=(k == J - 1))
                    if k == J - 1:
                        mm.then_inc(xdbl_done, 1)

            def before_softplus(c, th, j, wait):
                e.wait_ge(dtrows_done, 1 + c + 1)
                e.wait_ge(evac[S], 1 + wait)
                e.matmul(dense[:, S, :], dtw[0:DR + 1, j * P:(j + 1) * P], dtaug[:, th, :], start=True, stop=True) \
                    .then_inc(v_done, 1)

            def sum_pair(g, q):
                e.wait_ge(prod_done, 1 + 1 + PAIRS * g + q + 1)
                for i in (0, 1):
                    for k in range(TB):
                        mm = e.matmul(yT[:, k, :], h[:, 2 * (q % RH) + i, k * P:(k + 1) * P], ident[:],
                                      is_transpose=True, start=False, stop=(q == PAIRS - 1 and i == 1),
                                      skip_group_check=True)
                mm.then_inc(prod_summed, 1)

            e.wait_ge(ctx_loaded, 1 + 16)
            for G in range(J):
                in_proj(G // 2 + 1, G % 2, G % 2, G // 2)
            e.wait_ge(const_loaded, 1 + 16 * CONSTS)
            e.wait_ge(masks, 1 + MASKS)
            e.wait_ge(ident_step, 3)
            x_proj(0, 0, J // 2)
            x_proj_part(0, range(J // 2, J))
            e.wait_ge(ctx_loaded, 1 + 32)
            for G in range(J, AHEAD):
                in_proj(G // 2 + 1, G % 2, G % 2, G // 2 + (1 - G % 2))
            before_softplus(0, 0, 0, AHEAD // 2 + 1)

            def slot(b, plan, t):
                st, q = divmod(t, SLOTS)
                g, c = STEPS * b + st, TH * b + st // J
                th, j = divmod(st, J)
                if late(plan, t, 0):
                    sum_pair(g - 1, PAIRS - 1)
                for what, *a in plan.slots[t]:
                    name = (what, *a)
                    if what == "in_proj":
                        if (st + AHEAD) % J == 0:
                            e.wait_ge(ctx_loaded, 1 + 16 * (TH * b + (st + AHEAD) // J + 1))
                        in_proj(STEPS // 2 * b + (st + AHEAD) // 2 + 1, (st + AHEAD) % 2, S, count(plan, b, name))
                    elif what == "x_proj":
                        x_proj(c + 1, 1 - th, count(plan, b, name))
                    elif what == "x_proj_end":
                        x_proj_part(1 - th, range(J // 2, J))
                    elif what == "zT":
                        e.wait_ge(zn_done, 1 + g + 1)
                        e.wait_ge(evac[S], 1 + count(plan, b, name))
                        for k in range(TB):
                            mm = e.transpose(dense[:, S, k * P:(k + 1) * P], xz[:, k * P:(k + 1) * P], ident[:])
                        mm.then_inc(zT_done, 1)
                    elif what == "v":
                        bo, th2, j2 = chunk_block(st + 1)
                        before_softplus(TH * (b + bo) + th2, th2, j2, count(plan, b, name))
                if plan.scan:
                    if q == 1:
                        e.wait_ge(yg_done, 1 + g)
                        e.wait_ge(Dd_done, 1 + g + 1)
                        for k in range(TB):
                            e.matmul(yT[:, k, :], u[:, st, k * P:(k + 1) * P], Dd[:], start=(k == 0), stop=False,
                                     skip_group_check=True)
                    if q >= 1:
                        sum_pair(g, q - 1)
                for what, *a in plan.slots[t]:
                    name = (what, *a)
                    if what == "logit":
                        k, i, bank = a
                        f = f_index(logit_batch(b, k), k)
                        if i == 0:
                            e.wait_ge(norm_done, 1 + f + 1)
                            e.wait_ge(evac[bank], 1 + count(plan, b, ("logit", k)))
                        ring = sw_bufs(k)
                        e.wait_ge(sw_sem(k)[i % ring], 1 + 16 * ((TB * logit_batch(b, k) + k % TB)
                                                                 * len(range(i % ring, SWL, ring)) + i // ring + 1))
                        p = row_at(plan, b, ("logits", k))[0]
                        for n in range(SD // 32):
                            lo = i * SD + 32 * n
                            mm = e.matmul(dense[32 * n:32 * n + 32, bank, 0:32 * E], row[:, p, lo:lo + 32],
                                          sw_ring[i % ring][:, :, 32 * n:32 * n + 32],
                                          start=(i == 0), stop=(i == SWL - 1))
                        mm.then_inc(sw_used, 1)
                    elif what == "logit_sum":
                        e.wait_ge(lgr_done, 1 + 2 * TB * b)
                        e.wait_ge(evac[F2], 1 + count(plan, b, name))
                        for k in range(2 * TB):
                            mm = e.matmul(dense[:, F2, 0:E], ones[:], lgr[:, k, :], start=(k == 0),
                                          stop=(k == 2 * TB - 1))
                        mm.then_inc(lg_done, 1)
                    elif what == "turn":
                        uu, k = a
                        f = 2 * TB * (b - 1) + TB * uu + k
                        p = row_at(plan, b, name)[0]
                        e.wait_ge(renorm_done, 1 + f + 1)
                        for i in (0, 1):
                            e.wait_ge(evac[F0 + i], 1 + count(plan, b, (*name, i)))
                            for n in range(J // 2):
                                d = (J // 2) * i + n
                                mm = e.transpose(dense[:, F0 + i, n * P:(n + 1) * P], row[:, p, d * P:(d + 1) * P],
                                                 ident[:])
                            mm.then_inc(tr_done, 1)
                    elif what == "hidden":
                        uu, hp = a
                        if hp == 0:
                            e.wait_ge(sel_step, 1 + 9 * b)
                            for i in (0, 1):
                                last = ("turn", uu, TB - 1, i)
                                e.wait_ge(evac[F0 + i], 1 + count(plan, b, last) + 1)
                        for i in (0, 1):
                            e.wait_ge(evac[F0 + i], 1 + count(plan, b, (*name, i)))
                            e.matmul(dense[:, F0 + i, :], w1s[HD * i:HD * i + HD].rearrange("p k f -> p (k f)"),
                                     xT[HD * i:HD * i + HD, hp, :], start=True, stop=True).then_inc(hid_done, 1)
                    elif what == "expert_out":
                        uu, hp = a
                        for i in (0, 1):
                            e.wait_ge(evac[F0 + i], 1 + count(plan, b, ("hidden", uu, hp, i)) + 1)
                        e.wait_ge(evac[F2], 1 + count(plan, b, name))
                        for i in (0, 1):
                            mm = e.matmul(dense[HD * i:HD * i + HD, F2, :], w2s[:], hs[:, i, :],
                                          start=True, stop=True)
                        mm.then_inc(o_done, 1)
                    elif what == "tile":
                        uu, i, k = a
                        bank = bank_of(plan, ("tile", uu, i))
                        if k == 0:
                            if i == 0:
                                e.wait_ge(evac[F2], 1 + count(plan, b, ("expert_out", uu, J - 1)) + 1)
                            e.wait_ge(w3_loaded[i % 2], 1 + 16 * (NQ * (b - 1) + NQ // 2 * uu + i // 2 + 1))
                            e.wait_ge(evac[bank], 1 + count(plan, b, ("tile", uu, i)))
                        part = dense[:, bank, k * QD:(k + 1) * QD]
                        e.matmul(part, ones[B3:B3 + 1, :], dtw[B3:B3 + 1, i * QD:(i + 1) * QD],
                                 start=True, stop=False)
                        for d in range(J):
                            mm = e.matmul(part, xT[:, d, k * P:(k + 1) * P], w3q[:, i % 2, d, :],
                                          start=False, stop=(d == J - 1))
                        if k == TB - 1:
                            mm.then_inc(w3_done, 1)
            turns(e, slot)

        @block.scalar
        def _(act):
            e = act
            e.wait_ge(const_loaded, 1 + 16 * CONSTS)
            e.activation(Av[:], Av[:], ACT.Exp).then_inc(a_ready, 1)

            def pad(G, bank):
                e.wait_ge(conv_step, 1 + 6 * G)
                e.wait_ge(xin_done, 1 + 1 + G + 1)
                e.copy(xpad[:, DC - 1:CH], dense[:, bank, :]).then_inc(evac[bank], 1)

            def silu_u(G, slot_u):
                e.wait_ge(conv_step, 1 + 6 * G + 5)
                e.activation(u[:, slot_u, :], cacc[:], ACT.Silu).then_inc(u_done, 1)

            def split_rows(c, th):
                e.wait_ge(xdbl_done, 1 + c + 1)
                e.copy(dtaug[0:DR, th, :], dense[0:DR, S, :]).then_inc(dtrows_done, 1)
                e.copy(bcs, dense[DR:DR + 2 * N, S, :]).then_inc(evac[S], 1)

            def softplus_a(g, p):
                e.wait_ge(v_done, 1 + g + 1)
                e.activation(delta[:, p, :], dense[:, S, :], ACT.Abs).then_inc(sp_step, 1)
                e.wait_ge(sp_step, 1 + 3 * g + 1)
                e.activation(delta[:, p, :], delta[:, p, :], ACT.Exp, scale=-1.0).then_inc(sp_step, 1)

            def softplus_b(g, p):
                e.wait_ge(sp_step, 1 + 3 * g + 2)
                e.activation(delta[:, p, :], delta[:, p, :], ACT.Ln, bias=1.0).then_inc(sp_step, 1)

            def exp_ln_table():
                e.preload_act_table_set("natural_log_exp_and_others")

            for G in range(J):
                pad(G, G % 2)
                silu_u(G, G)
            split_rows(0, 0)
            for G in range(J, AHEAD):
                pad(G, G % 2)
                silu_u(G, G)
            e.wait_ge(masks, 1 + MASKS)
            softplus_a(0, 0)
            softplus_b(0, 0)
            e.wait_ge(a_ready, 3)

            def slot(b, plan, t):
                st, q = divmod(t, SLOTS)
                g, c = STEPS * b + st, TH * b + st // J
                if late(plan, t, 2):
                    e.wait_ge(x1_done, 1 + g - 1)
                    if plan.scan:
                        e.wait_ge(du_done, 1 + g - 1)
                        silu_u(g - 1 + AHEAD, (st - 1 + AHEAD) % UR)
                    e.wait_ge(zT_done, 1 + g)
                    e.activation(szT[:].rearrange("p k e -> p (k e)"), dense[:, S, :], ACT.Silu) \
                        .then_inc(evac[S], 1)
                    exp_ln_table()
                if plan.scan:
                    th, j = divmod(st, J)
                    if q == 0:
                        e.wait_ge(prod_summed, 1 + PAIRS * g + 1)
                        e.activation(Dd[:], ident[:], ACT.Copy, scale=Dv[:, j:j + 1]).then_inc(Dd_done, 1)
                        if plan is FIRST and st == 0:
                            e.wait_ge(evac[S], 1 + LEAD_USES[S])
                        else:
                            e.wait_ge(evac[S], 1 + filled_last_step(plan, b, st, "v"))
                    for n in (2 * q, 2 * q + 1):
                        e.wait_ge(h_done, 1 + N * g + n)
                        e.activation(dA[:, n % RA, :], delta[:, st % 2, :], ACT.Exp,
                                     scale=Av[:, j * N + n:j * N + n + 1]).then_inc(dA_done, 1)
                    if q == 3:
                        if st == 0:
                            e.wait_ge(ln1_done, 1 + b + 1)
                        e.wait_ge(xz_loaded, 1 + 16 * (g + 1))
                        e.activation(xz[:], xz[:], ACT.Identity, scale=r1[:, j:j + 1], bias=nm1[:, j:j + 1]) \
                            .then_inc(zn_done, 1)
                    if q == 4:
                        softplus_a(g + 1, (st + 1) % 2)
                        softplus_b(g + 1, (st + 1) % 2)
                    if q == 6 and j == J - 2:
                        split_rows(c + 1, 1 - th)
                    if q == 7:
                        pad(g + AHEAD, S)
                for what, *a in plan.slots[t]:
                    name = (what, *a)
                    if what == "norm":
                        k = a[0]
                        f = f_index(logit_batch(b, k), k)
                        p = row_at(plan, b, ("logits", k))[0]
                        e.wait_ge(nm_done, 1 + f + 1)
                        e.activation(row[:, p, :], row[:, p, :], ACT.Identity, scale=r2[:, k:k + 1],
                                     bias=nm2[:, k:k + 1]).then_inc(norm_done, 1)
                    elif what == "route":
                        e.wait_ge(route_step, 1 + 5 * (b - 1) + 2)
                        e.activation(rt[:, 1, :], rt[:, 0, :], ACT.Exp, bias=rt[:, 6, 0:1],
                                     accum_out=rt[:, 6, 1:2]).then_inc(pexp_done, 1)
                    elif what == "renorm":
                        uu, k = a
                        f = 2 * TB * (b - 1) + TB * uu + k
                        p, filled = row_at(plan, b, ("turn", uu, k))
                        e.wait_ge(row_loaded[p], 1 + 16 * (filled + 1))
                        e.activation(row[:, p, :], row[:, p, :], ACT.Identity, scale=r2[:, TB * uu + k:TB * uu + k + 1],
                                     bias=nm2[:, TB * uu + k:TB * uu + k + 1]).then_inc(renorm_done, 1)
                    elif what == "turned":
                        uu, k = a
                        f = 2 * TB * (b - 1) + TB * uu + k
                        for i in (0, 1):
                            e.wait_ge(tr_done, 1 + 2 * f + i + 1)
                            e.wait_ge(w3_done, 1 + 1 + 2 * NQ * (b - 1) + NQ * uu)
                            e.copy(xT[:, (J // 2) * i:(J // 2) * (i + 1), k * P:(k + 1) * P],
                                   dense[:, F0 + i, :].rearrange("p (d t) -> p d t", t=P)).then_inc(evac[F0 + i], 1)
                    elif what == "gelu":
                        uu, hp = a
                        n = 2 * J * (b - 1) + J * uu + hp
                        e.wait_ge(o_done, 1 + n)
                        if hp == 0:
                            e.wait_ge(sel_step, 1 + 9 * b)
                        for i in (0, 1):
                            e.wait_ge(hid_done, 1 + 2 * n + i + 1)
                            e.activation(hs[:, i, :], dense[:, F0 + i, :], ACT.Gelu, bias=b1s[:]) \
                                .then_inc(evac[F0 + i], 1)
                        if plan.scan:
                            exp_ln_table()
            turns(e, slot)

        @block.vector
        def _(dve):
            e = dve
            e.memset(ones[:], 1.0).then_inc(masks, 1)
            e.memset(half[:, 0:1], -0.5).then_inc(masks, 1)
            e.memset(dtaug[DR:DR + 1], 1.0).then_inc(masks, 1)
            for i in range(E):
                e.memset(iota[:, i:i + 1], float(i)).then_inc(set_up, 1)
            e.wait_ge(ident_step, 3)
            e.wait_ge(set_up, 1 + E)
            e.tensor_copy(diag[:], ident[:, 0:32]).then_inc(set_up, 1)
            for i in range(1, 4):
                e.wait_ge(set_up, 1 + E + i)
                e.tensor_tensor(diag[:], diag[:], ident[:, 32 * i:32 * i + 32], ALU.add).then_inc(set_up, 1)
            e.wait_ge(a_ready, 2)
            e.tensor_scalar(Av[:], Av[:], -1.0, None, ALU.mult).then_inc(a_ready, 1)

            def conv_a(G, bank, evacs, th, j, stored):
                if j == 0:
                    e.wait_ge(bc_stored, 1 + stored)
                    settle(e)
                if th == 0:
                    e.memset(xpad[:, 0:DC - 1], 0.0).then_inc(conv_step, 1)
                else:
                    e.tensor_copy(xpad[:, 0:DC - 1], halo[:, j, :]).then_inc(conv_step, 1)
                e.wait_ge(evac[bank], 1 + evacs)
                e.wait_ge(u_done, 1 + G)
                e.tensor_scalar(cacc[:], xpad[:, DC - 1:CH], cw[:, j, DC - 1:DC], cb[:, j:j + 1],
                                ALU.mult, ALU.add).then_inc(conv_step, 1)
                tap(G, 2, j)

            def tap(G, k, j):
                e.wait_ge(conv_step, 1 + 6 * G + DC - k)
                e.scalar_tensor_tensor(out=cacc[:], in0=xpad[:, k:k + T], scalar=cw[:, j, k:k + 1], in1=cacc[:],
                                       op0=ALU.mult, op1=ALU.add).then_inc(conv_step, 1)

            def conv_b(G, j):
                tap(G, 1, j)
                tap(G, 0, j)
                e.tensor_copy(halo[:, j, :], xpad[:, T:CH]).then_inc(conv_step, 1)
                e.wait_ge(conv_step, 1 + 6 * G + 6)

            def ln1_stats(b, k, p, filled):
                n = 3 * J * b + 3 * k
                e.wait_ge(row_loaded[p], 1 + 16 * (filled + 1))
                e.bn_stats(bst[:, 0, :], row[:, p, 0:T]).then_inc(ln1_step, 1)
                e.bn_stats(bst[:, 1, :], row[:, p, T:DI]).then_inc(row_free[p], 1)
                e.wait_ge(ln1_step, 1 + n + 1)
                e.wait_ge(row_free[p], 1 + filled + 1)
                settle(e)
                e.bn_aggr(mv1[:, k, :], bst[:].rearrange("p a b -> p (a b)")).then_inc(ln1_step, 1)
                e.wait_ge(ln1_step, 1 + n + 2)
                e.tensor_scalar(mv1[:, k, 1:2], mv1[:, k, 1:2], EPS, None, ALU.add).then_inc(ln1_step, 1)
                e.wait_ge(ln1_step, 1 + n + 3)

            def ln1_shift(b):
                e.wait_ge(ln1_rs, 1 + b + 1)
                e.scalar_tensor_tensor(out=nm1[:], in0=mv1[:, :, 0], scalar=-1.0, in1=r1[:], op0=ALU.mult,
                                       op1=ALU.mult).then_inc(ln1_done, 1)
                e.wait_ge(ln1_done, 1 + b + 1)

            def softplus_c(g, p, waits):
                e.wait_ge(sp_step, 1 + 3 * g + 3)
                e.scalar_tensor_tensor(out=delta[:, p, :], in0=dense[:, S, :], scalar=0.0, in1=delta[:, p, :],
                                       op0=ALU.max, op1=ALU.add).then_inc(evac[S], 1)
                e.wait_ge(evac[S], 1 + waits + 1)

            for G in range(AHEAD):
                evacs = G // 2 + 1 + (1 if G >= J and G % 2 == 0 else 0)
                conv_a(G, G % 2, evacs, G // J, G % J, 16 * (G // J))
                conv_b(G, G % J)
                if G >= 2:
                    ln1_stats(0, G - 2, G % 2, (G - 2) // 2)
            ln1_shift(0)
            softplus_c(0, 0, AHEAD // 2 + 1)

            def slot(b, plan, t):
                st, q = divmod(t, SLOTS)
                g, c = STEPS * b + st, TH * b + st // J
                th, j = divmod(st, J)
                if plan.scan and late(plan, t, 0):
                    conv_b(g - 1 + AHEAD, (st - 1 + AHEAD) % J)
                if late(plan, t, 2):
                    e.wait_ge(evac[S], 1 + filled_last_step(plan, b, st, "zT"))
                    e.wait_ge(prod_summed, 1 + PAIRS + PAIRS * g)
                    e.tensor_tensor(szT[:], yT[:], szT[:], ALU.mult).then_inc(yg_done, 1)
                for what, *a in plan.slots[t]:
                    name = (what, *a)
                    if what == "stats":
                        k = a[0]
                        f = f_index(logit_batch(b, k), k)
                        p, filled = row_at(plan, b, ("logits", k))
                        e.wait_ge(row_loaded[p], 1 + 16 * (filled + 1))
                        for i in (0, 1):
                            e.bn_stats(bst[:, i, :], row[:, p, i * T:(i + 1) * T]).then_inc(mv_step, 1)
                        e.wait_ge(mv_step, 1 + 4 * f + 2)
                        settle(e)
                        e.bn_aggr(mv[:], bst[:].rearrange("p a b -> p (a b)")).then_inc(mv_step, 1)
                        e.wait_ge(mv_step, 1 + 4 * f + 3)
                        e.tensor_scalar(mv[:, 1:2], mv[:, 1:2], EPS, None, ALU.add).then_inc(mv_step, 1)
                    elif what == "shift":
                        k = a[0]
                        f = f_index(logit_batch(b, k), k)
                        e.wait_ge(rs_done, 1 + f + 1)
                        e.scalar_tensor_tensor(out=nm2[:, k:k + 1], in0=mv[:, 0:1], scalar=-1.0,
                                               in1=r2[:, k:k + 1], op0=ALU.mult, op1=ALU.mult).then_inc(nm_done, 1)
                        e.wait_ge(nm_done, 1 + f + 1)
                    elif what == "diagonal":
                        k = a[0]
                        f = f_index(logit_batch(b, k), k)
                        bank = bank_of(plan, ("logit", k))
                        e.wait_ge(sw_used, 1 + SW0 + SWL * (f + 1))
                        p, filled = row_at(plan, b, ("logits", k))
                        e.sem_inc(row_free[p], 1)
                        e.tensor_tensor(lgm[:], dense[:, bank, 0:32 * E].rearrange("p (e i) -> p e i", i=32),
                                        diag[:].unsqueeze(1).broadcast_to([P, E, 32]), ALU.mult) \
                            .then_inc(evac[bank], 1)
                        e.wait_ge(evac[bank], 1 + count(plan, b, ("logit", k)) + 1)
                        e.tensor_reduce(lgr[:, k, :], lgm[:], AX.X, ALU.add).then_inc(lgr_done, 1)
                        e.wait_ge(lgr_done, 1 + f + 1)
                    elif what == "turned":
                        f = 2 * TB * (b - 1) + TB * a[0] + a[1]
                        e.wait_ge(tr_done, 1 + 2 * f + 2)
                        e.sem_inc(row_free[row_at(plan, b, ("turn", *a))[0]], 1)
                    elif what == "route":
                        route(b, count(plan, b, ("logit_sum",)))
                    elif what == "out_add":
                        uu, hp = a
                        e.wait_ge(o_done, 1 + 2 * J * (b - 1) + J * uu + hp + 1)
                        e.scalar_tensor_tensor(out=xT[:, hp, :], in0=dense[:, F2, :], scalar=b2s[:], in1=xT[:, hp, :],
                                               op0=ALU.add, op1=ALU.add).then_inc(evac[F2], 1)
                    elif what == "tile_out":
                        uu, i = a
                        bank = bank_of(plan, ("tile", uu, i))
                        e.wait_ge(w3_done, 1 + 1 + 2 * NQ * (b - 1) + NQ * uu + i + 1)
                        e.wait_ge(res_loaded[i % 2], 1 + 16 * (NQ * (b - 1) + NQ // 2 * uu + i // 2 + 1))
                        e.tensor_tensor(res[:, i % 2], dense[:, bank, :].rearrange("p (k d) -> p k d", d=QD),
                                        res[:, i % 2], ALU.add).then_inc(evac[bank], 1)
                    elif what == "ln1_stats":
                        ln1_stats(b + 1, a[0], *row_at(plan, b, ("ln1", a[0])))
                    elif what == "ln1_shift":
                        ln1_shift(b + 1)
                if not plan.scan:
                    return
                if q == SLOTS - 1:
                    conv_a(g + AHEAD, S, count(plan, b, ("in_proj", st)) + 1, (st + AHEAD) // J % TH, (st + AHEAD) % J,
                           16 * (c + 2))

                def bank(n):
                    return (N * st + n) % 3

                def times_b(n):
                    e.wait_ge(h_done, 1 + RA - 1 + N * g + (0 if st == 0 and n == 0 else n - 2))
                    if j == 0 and n % 2 == 0:
                        e.wait_ge(bc_loaded[n // 2], 1 + 32 * (c + 1))
                    e.tensor_tensor(duB[:, bank(n), :], du[:], Bb[:, n, :], ALU.mult).then_inc(duB_done, 1)

                if q == 0:
                    e.tensor_tensor(du[:], delta[:, st % 2, :], u[:, st, :], ALU.mult).then_inc(du_done, 1)
                    e.wait_ge(du_done, 1 + g + 1)
                    times_b(0)
                for n in (2 * q, 2 * q + 1):
                    if n + 1 < N:
                        times_b(n + 1)
                    e.wait_ge(duB_done, 1 + N * g + n + 1)
                    e.wait_ge(dA_done, 1 + N * g + n + 1)
                    if n % 2 == 0:
                        e.wait_ge(prod_summed, 1 + PAIRS + PAIRS * g + (q - RH + 1 if q >= RH else min(q - 1, 0)))
                    if th:
                        e.wait_ge(saved, 1 + PAIRS * (J * (b + 1)))
                    e.tensor_tensor_scan(h[:, 2 * (q % RH) + n % 2, :], dA[:, n % RA, :], duB[:, bank(n), :],
                                         state[:, j * N + n:j * N + n + 1] if th else 0.0, ALU.mult, ALU.add) \
                        .then_inc(h_done, 1)
                if q == SLOTS // 2:
                    softplus_c(g + 1, (st + 1) % 2, count(plan, b, ("v", st)))

            def route(b, before):
                r, n = 5 * (b - 1), 9 * (b - 1)
                e.wait_ge(lg_done, 1 + b)
                e.tensor_tensor(rt[:, 0, :], dense[:, F2, 0:E], swb[:], ALU.add).then_inc(evac[F2], 1)
                e.wait_ge(evac[F2], 1 + before + 1)
                settle(e)
                e.max(rt[:, 4, :], rt[:, 0, :]).then_inc(route_step, 1)
                e.wait_ge(route_step, 1 + r + 1)
                e.tensor_scalar(rt[:, 6, 0:1], rt[:, 4, 0:1], -1.0, None, ALU.mult).then_inc(route_step, 1)
                e.wait_ge(pexp_done, 1 + b)
                e.reciprocal(rt[:, 6, 2:3], rt[:, 6, 1:2]).then_inc(route_step, 1)
                e.wait_ge(route_step, 1 + r + 3)
                e.tensor_scalar(rt[:, 2, :], rt[:, 1, :], rt[:, 6, 2:3], None, ALU.mult).then_inc(route_step, 1)
                e.wait_ge(route_step, 1 + r + 4)
                settle(e)
                e.max(rt[:, 3, :], rt[:, 2, :]).then_inc(route_step, 1)
                e.wait_ge(route_step, 1 + r + 5)
                settle(e)
                e.max_index(idx[:], rt[:, 3, :], rt[:, 2, :]).then_inc(top_step, 1)
                e.wait_ge(top_step, 1 + 9 * (b - 1) + 1)
                e.tensor_copy(rt[:, 5, :], idx[:]).then_inc(top_step, 1)
                e.wait_ge(top_step, 1 + 9 * (b - 1) + 2)
                for i in (0, 1):
                    e.tensor_scalar(hot[:, i, :], iota[:], rt[:, 5, i:i + 1], None, ALU.is_equal).then_inc(top_step, 1)
                    lo = HD * i
                    e.tensor_scalar(hot[lo:lo + HD, 2, :], iota[lo:lo + HD], rt[lo:lo + HD, 5, i:i + 1], None,
                                    ALU.is_equal).then_inc(top_step, 1)
                    e.tensor_scalar(hot[lo:lo + HD, 3, :], iota[lo:lo + HD], rt[lo:lo + HD, 5, i:i + 1],
                                    rt[lo:lo + HD, 3, i:i + 1], ALU.is_equal, ALU.mult).then_inc(top_step, 1)
                e.wait_ge(top_step, 1 + 9 * (b - 1) + 8)
                e.tensor_scalar(rt[:, 4, :], hot[:, 0, :], rt[:, 3, 0:1], None, ALU.mult).then_inc(top_step, 1)
                e.wait_ge(top_step, 1 + 9 * (b - 1) + 9)
                e.scalar_tensor_tensor(out=rt[:, 4, :], in0=hot[:, 1, :], scalar=rt[:, 3, 1:2], in1=rt[:, 4, :],
                                       op0=ALU.mult, op1=ALU.add).then_inc(sel_step, 1)
                e.wait_ge(experts_loaded, 1 + 64 * b)
                done = 1
                for src, on, dst in ((w12[:, 0], hot[:, 0, :], w1s[:, 0, :]), (w12[:, 0], hot[:, 1, :], w1s[:, 1, :]),
                                     (w12[:, 1], hot[:, 3, :], w2s[:])):
                    e.wait_ge(sel_step, 1 + n + done)
                    e.tensor_tensor(wt, src, on.unsqueeze(2).broadcast_to([P, E, HD]), ALU.mult) \
                        .then_inc(sel_step, 1)
                    e.wait_ge(sel_step, 1 + n + done + 1)
                    e.tensor_reduce(dst, wt.rearrange("p e f -> p f e"), AX.X, ALU.add).then_inc(sel_step, 1)
                    done += 2
                e.tensor_tensor_reduce(lgm[:, :, 0], b1c[:], hot[:, 2, :], 1.0, 0.0, ALU.mult, ALU.add,
                                       b1s[:]).then_inc(sel_step, 1)
                e.wait_ge(sel_step, 1 + n + 8)
                e.tensor_tensor_reduce(lgm[:, :, 0], b2c[:], rt[:, 4, :], 1.0, 0.0, ALU.mult, ALU.add,
                                       b2s[:]).then_inc(sel_step, 1)
                e.wait_ge(sel_step, 1 + n + 9)

            turns(e, slot)


def kernel(**inputs):
    import numpy as _np
    import concourse.bacc as _bacc
    from concourse import mybir as _mybir
    from concourse.bass_utils import run_bass_kernel_spmd as _run

    def get(name):
        return _np.asarray(inputs[name])

    laid = {
        "x": get("x"),
        "ctxT": get("ctx_1024").transpose(0, 2, 1),
        "w_inT": get("L0_xattn_in_proj_w").reshape(J, P, DK, P).transpose(0, 3, 2, 1),
        "conv_w": get("L0_xattn_conv_w"),
        "conv_b": get("L0_xattn_conv_b"),
        "x_projT": get("L0_xattn_x_proj_w").T,
        "dt_projT": get("L0_xattn_dt_proj_w").T,
        "dt_b": get("L0_xattn_dt_proj_b").reshape(1, -1),
        "A_log": get("L0_xattn_A_log"),
        "D": get("L0_xattn_D"),
        "sw": get("L0_ffn_switch_w").reshape(E, L, DI // SD, SD).transpose(1, 2, 0, 3),
        "sw_b": get("L0_ffn_switch_b"),
        "w1T": get("L0_ffn_w1").transpose(0, 2, 1),
        "b1": get("L0_ffn_b1"),
        "w2T": get("L0_ffn_w2").transpose(0, 2, 1),
        "b2": get("L0_ffn_b2"),
        "w3T": get("L0_ffn_w3").reshape(NQ, QD, J, P).transpose(0, 3, 2, 1),
        "b3": get("L0_ffn_b3"),
    }
    nc = _bacc.Bacc("TRN2", target_bir_lowering=False, num_devices=1)
    arrays, args = {}, []
    for name, a in laid.items():
        a = _np.ascontiguousarray(a)
        arrays[f"in_{name}"] = a
        args.append(nc.dram_tensor(f"in_{name}", a.shape, _mybir.dt.from_np(a.dtype), kind="ExternalInput").ap())
    args.append(nc.dram_tensor("out_0", (NB, L, DI), _mybir.dt.float32, kind="ExternalOutput").ap())
    build(nc, *args)
    r = _run(nc, [arrays], core_ids=[0])
    return r.results[0]["out_0"]
```
